# Optimizing a Trainium2 kernel written in Bass

```python
import numpy as np
import jax
import jax.numpy as jnp

def _softmax(x, axis=-1):
    return jax.nn.softmax(x, axis=axis)

def _gelu(x):
    return jax.nn.gelu(x, approximate=True)

def _silu(x):
    return jax.nn.silu(x)

def _sigmoid(x):
    return jax.nn.sigmoid(x)

def _layernorm(x, axis=-1, eps=1e-05):
    m = jnp.mean(x, axis=axis, keepdims=True)
    v = jnp.var(x, axis=axis, keepdims=True)
    return (x - m) / jnp.sqrt(v + eps)

def _scatter_add(tgt, idx, src, axis=0):
    return tgt.at[idx].add(src)

def _segment_sum(src, seg, n):
    return jax.ops.segment_sum(src, seg, n)
kernel_name = 'mk_gnn_resnorm_d1_gnn_r32_950bf6'

def setup_inputs(seed: int=0):
    np.random.seed(seed)
    _w = jnp.asarray

    def _rec_inputs():
        import jax
        import jax.numpy as jnp
        _gk = jax.random.key(seed)
        x = -0.000202 + 1 * jax.random.normal(jax.random.fold_in(_gk, 1), (50000, 128), jnp.float32)
        src = jax.random.randint(jax.random.fold_in(_gk, 2), (50000,), 0, 50000, jnp.int32)
        dst = jnp.minimum((50000 * jax.random.uniform(jax.random.fold_in(_gk, 3), (50000,)) ** 2.0).astype(jnp.int32), 49999)
        _o = jnp.argsort(dst, stable=True)
        src = src[_o]
        dst = dst[_o]
        edge_attr_3 = -0.000451519 + 1.00018 * jax.random.normal(jax.random.fold_in(_gk, 12), (50000, 3), jnp.float32)
        edge_weight = jax.random.uniform(jax.random.fold_in(_gk, 13), (50000,), jnp.float32, 0.0, 0.999998)
        return (x, src, dst, edge_attr_3, edge_weight)
    x, src, dst, edge_attr_3, edge_weight = _rec_inputs()

    def _L0_gnn_setup():
        import jax, jax.numpy as jnp
        import numpy as np
        N = 50000
        E = 25000
        MUL = 32
        NB = 8
        R_MAX = 1.0
        AVG = 16.0
        SQ3 = 3.0 ** 0.5

        def _radial_embedding(r):
            x = jnp.clip(r / R_MAX, 0.0, 1.0)
            centers = jnp.arange(NB, dtype=jnp.float32) / (NB - 1)
            sigma = 1.0 / (NB - 1)
            emb = jnp.exp(-0.5 * ((x[:, None] - centers[None, :]) / sigma) ** 2)
            emb = emb * NB ** 0.5 * (r <= R_MAX).astype(jnp.float32)[:, None]
            return emb
        key = jax.random.key(seed)
        k = jax.random.split(key, 12)
        inp = {'node_feats': jax.random.normal(k[0], (N, 4 * MUL), dtype=jnp.float32), 'edge_vec': jax.random.normal(k[1], (E, 3), dtype=jnp.float32), 'edge_length': jax.random.uniform(k[2], (E,), dtype=jnp.float32), 'senders': jax.random.randint(k[3], (E,), 0, N, dtype=jnp.int32), 'receivers': jax.random.randint(k[4], (E,), 0, N, dtype=jnp.int32), 'num_nodes': N, 'W_up0': jax.random.normal(k[5], (MUL, MUL), dtype=jnp.float32), 'W_up1': jax.random.normal(k[6], (MUL, MUL), dtype=jnp.float32), 'mlp_w0': jax.random.normal(k[7], (NB, 64), dtype=jnp.float32) / NB ** 0.5, 'mlp_b0': jnp.zeros((64,), dtype=jnp.float32), 'mlp_w1': jax.random.normal(k[8], (64, 64), dtype=jnp.float32) / 8.0, 'mlp_b1': jnp.zeros((64,), dtype=jnp.float32), 'mlp_w2': jax.random.normal(k[9], (64, 4 * MUL), dtype=jnp.float32) / 8.0, 'mlp_b2': jnp.zeros((4 * MUL,), dtype=jnp.float32), 'W_out0': jax.random.normal(k[10], (2 * MUL, MUL), dtype=jnp.float32), 'W_out1': jax.random.normal(k[11], (2 * MUL, MUL), dtype=jnp.float32)}
        return inp
    _L0_gnn_all = _L0_gnn_setup()
    _L0_gnn_in = {k: v for k, v in _L0_gnn_all.items() if k in ('W_up0', 'W_up1', 'mlp_w0', 'mlp_b0', 'mlp_w1', 'mlp_b1', 'mlp_w2', 'mlp_b2', 'W_out0', 'W_out1')}
    del _L0_gnn_all
    return {'x': x, 'src': src, 'dst': dst, 'edge_attr_3': edge_attr_3, 'edge_weight': edge_weight, 'L0_gnn_W_up0': _L0_gnn_in['W_up0'], 'L0_gnn_W_up1': _L0_gnn_in['W_up1'], 'L0_gnn_mlp_w0': _L0_gnn_in['mlp_w0'], 'L0_gnn_mlp_b0': _L0_gnn_in['mlp_b0'], 'L0_gnn_mlp_w1': _L0_gnn_in['mlp_w1'], 'L0_gnn_mlp_b1': _L0_gnn_in['mlp_b1'], 'L0_gnn_mlp_w2': _L0_gnn_in['mlp_w2'], 'L0_gnn_mlp_b2': _L0_gnn_in['mlp_b2'], 'L0_gnn_W_out0': _L0_gnn_in['W_out0'], 'L0_gnn_W_out1': _L0_gnn_in['W_out1']}

def reference(x, src, dst, edge_attr_3, edge_weight, L0_gnn_W_up0, L0_gnn_W_up1, L0_gnn_mlp_w0, L0_gnn_mlp_b0, L0_gnn_mlp_w1, L0_gnn_mlp_b1, L0_gnn_mlp_w2, L0_gnn_mlp_b2, L0_gnn_W_out0, L0_gnn_W_out1):
    import jax
    import jax.numpy as jnp

    def _L0_gnn_ref(node_feats, edge_vec, edge_length, senders, receivers, num_nodes, W_up0, W_up1, mlp_w0, mlp_b0, mlp_w1, mlp_b1, mlp_w2, mlp_b2, W_out0, W_out1):
        import jax, jax.numpy as jnp
        import numpy as np
        N = 50000
        E = 25000
        MUL = 32
        NB = 8
        R_MAX = 1.0
        AVG = 16.0
        SQ3 = 3.0 ** 0.5

        def _radial_embedding(r):
            x = jnp.clip(r / R_MAX, 0.0, 1.0)
            centers = jnp.arange(NB, dtype=jnp.float32) / (NB - 1)
            sigma = 1.0 / (NB - 1)
            emb = jnp.exp(-0.5 * ((x[:, None] - centers[None, :]) / sigma) ** 2)
            emb = emb * NB ** 0.5 * (r <= R_MAX).astype(jnp.float32)[:, None]
            return emb
        f32 = jnp.float32
        rhat = edge_vec / (jnp.linalg.norm(edge_vec, axis=-1, keepdims=True) + 1e-12)
        Y1 = SQ3 * rhat
        emb = _radial_embedding(edge_length)
        h = jax.nn.silu(emb @ mlp_w0 + mlp_b0)
        h = jax.nn.silu(h @ mlp_w1 + mlp_b1)
        w = (h @ mlp_w2 + mlp_b2).reshape(-1, 4, MUL)
        s = node_feats[:, :MUL]
        v = node_feats[:, MUL:].reshape(-1, MUL, 3)
        xs = s @ W_up0 / f32(MUL) ** 0.5
        xv = jnp.einsum('nmc,mk->nkc', v, W_up1) / f32(MUL) ** 0.5
        ss = xs[senders]
        vv = xv[senders]
        m0 = w[:, 0] * ss
        m1 = w[:, 1][:, :, None] * ss[:, :, None] * Y1[:, None, :]
        m2 = w[:, 2][:, :, None] * vv
        m3 = w[:, 3] * (jnp.einsum('emc,ec->em', vv, Y1) / SQ3)
        mid_s = jnp.concatenate([m0, m3], axis=1)
        mid_v = jnp.concatenate([m1, m2], axis=1)
        msg_s = jax.ops.segment_sum(mid_s, receivers, num_segments=num_nodes)
        msg_v = jax.ops.segment_sum(mid_v, receivers, num_segments=num_nodes)
        out_s = msg_s @ W_out0 / f32(2 * MUL) ** 0.5
        out_v = jnp.einsum('nmc,mk->nkc', msg_v, W_out1) / f32(2 * MUL) ** 0.5
        out = jnp.concatenate([out_s, out_v.reshape(-1, 3 * MUL)], axis=1)
        return out / max(AVG, 1e-08)
    x = _layernorm(x + _L0_gnn_ref(x, edge_attr_3, edge_weight, src, dst, 50000, L0_gnn_W_up0, L0_gnn_W_up1, L0_gnn_mlp_w0, L0_gnn_mlp_b0, L0_gnn_mlp_w1, L0_gnn_mlp_b1, L0_gnn_mlp_w2, L0_gnn_mlp_b2, L0_gnn_W_out0, L0_gnn_W_out1), axis=-1)
    return x

_drawn_inputs = setup_inputs


def setup_inputs(seed=0):
    import zlib

    import numpy as np

    out = dict(_drawn_inputs(seed))
    spreads = {'L0_gnn_mlp_b0': (0.0, 0.8), 'L0_gnn_mlp_b1': (0.0, 0.8), 'L0_gnn_mlp_b2': (0.0, 0.8)}
    factors = {'edge_attr_3': 3.121,
     'edge_weight': 3.14,
     'L0_gnn_W_up0': 3.032,
     'L0_gnn_W_up1': 2.972,
     'L0_gnn_W_out0': 4.398}
    for name, (base, spread) in spreads.items():
        noise = np.random.default_rng([zlib.crc32(name.encode()), seed]).standard_normal(out[name].shape)
        drawn = base * np.exp(spread * noise) if base else spread * noise
        out[name] = jnp.asarray(drawn.astype(out[name].dtype))
    for name, factor in factors.items():
        out[name] = (out[name] * factor).astype(out[name].dtype)
    return out
```

```python
from contextlib import ExitStack

import concourse.bass as bass
from concourse import mybir
from concourse.alu_op_type import AluOpType as ALU

F32 = mybir.dt.float32
I32 = mybir.dt.int32
ACT = mybir.ActivationFunctionType
AX_X = mybir.AxisListType.X

P = 128
N = 50000
E = 50000
D = 128
MUL = 32
NB = 8
HID = 64
AVG = 16.0
EPS = 1e-5

PITCH = -(-E // P)
LAST = E - (P - 1) * PITCH
G = 4
UNITS = -(-PITCH // G)
UNITS += UNITS % 2
TILES = UNITS * G
LAG = 3
MIDW = 9 * MUL

ROWS = 13
CHUNK = P * ROWS
CHUNKS = N // CHUNK
REST = N - CHUNKS * CHUNK
ZCOLS = 5000
assert N * D % (P * ZCOLS) == 0 and CHUNKS % 2 == 0 and REST <= P


def bass_gnn(nc, x, src, dst, edge_vec, edge_len, W_up0, W_up1, w0, b0, w1, b1, w2, b2, W_out0, W_out1, out):
    acc = [nc.dram_tensor(f"acc{m}", (N + P, D), F32, kind="Internal").ap() for m in range(2)]

    ctx = ExitStack()
    with ctx:
        def sb(name, shape, dt=F32):
            return ctx.enter_context(nc.sbuf_tensor(name, shape, dt))

        def psum(name, shape):
            return ctx.enter_context(nc.psum_tensor(name, shape, F32))

        def sem(name):
            return ctx.enter_context(nc.semaphore(name))

        ident = sb("ident", [P, P])
        earlier = sb("earlier", [P, P])
        dump_row = sb("dump_row", [P, TILES], I32)
        dump_rowf = sb("dump_rowf", [P, G])
        zeros = sb("zeros", [P, ZCOLS])
        centers = sb("centers", [P, NB])
        up_raw = sb("up_raw", [P, D])
        up = sb("up", [P, D])
        mlp0 = sb("mlp0", [G * NB, 2, 2 * HID])
        mlp1 = sb("mlp1", [2 * HID, 2 * HID])
        mlp2 = sb("mlp2", [2 * HID, 2, D])
        bias0 = sb("bias0", [2 * HID, 1])
        bias1 = sb("bias1", [2 * HID, 1])
        bias2 = sb("bias2", [P, D])
        out_raw = sb("out_raw", [P, 2, 2 * MUL])
        outw = sb("outw", [P, 2, 2 * MUL])
        src_all = sb("src_all", [P, TILES], I32)
        dst_int = sb("dst_int", [P, TILES], I32)
        dst_all = sb("dst_all", [P, TILES])
        row_all = sb("row_all", [P, TILES], I32)
        vec_all = sb("vec_all", [P, TILES, 3])
        vec_sq = sb("vec_sq", [P, TILES, 3])
        norm = sb("norm", [P, TILES])
        len_all = sb("len_all", [P, TILES])
        len_clip = sb("len_clip", [P, TILES])
        basis_all = sb("basis_all", [P, TILES, NB])
        src_now = sb("src_now", [P, 2, G], I32)
        row_now = sb("row_now", [P, 2, G], I32)
        sender = sb("sender", [P, 2, G, D])
        basis = sb("basis", [P, 2, G * NB])
        dst_now = sb("dst_now", [P, 2, G])
        basisT = sb("basisT", [G * NB, 2, P])
        senderT = sb("senderT", [P, 2, G * P])
        hid0 = sb("hid0", [2 * HID, 2, 2 * P])
        hid1 = sb("hid1", [2 * HID, 2, 2 * P])
        same = sb("same", [P, 2, G, P])
        junk = sb("junk", [P, 2, G, P])
        count = sb("count", [P, 2, G])
        rowf = sb("rowf", [P, 2, G])
        wts = sb("wts", [P, 2, G, D])
        mid = sb("mid", [P, 2, G, MIDW])
        proj = sb("proj", [P, 2, G, 3 * MUL])
        dot = sb("dot", [P, 2, G, MUL])
        sumT = sb("sumT", [P, 2, G, 2, P])
        msg = sb("msg", [P, 2, G, D])
        part0 = sb("part0", [P, 2, ROWS, D])
        part1 = sb("part1", [P, 2, ROWS, D])
        total = sb("total", [P, 2, ROWS, D])
        normed = sb("normed", [P, 2, ROWS, D])
        stats = sb("stats", [P, 2, ROWS, 6])
        mean = sb("mean", [P, 2, ROWS])
        half_gap = sb("half_gap", [P, 2, ROWS])
        gap_sq = sb("gap_sq", [P, 2, ROWS])
        var = sb("var", [P, 2, ROWS])
        std = sb("std", [P, 2, ROWS])
        rstd = sb("rstd", [P, 2, ROWS])
        shift = sb("shift", [P, 2, ROWS])
        eps = sb("eps", [P, 1])

        ps_hid = psum("ps_hid", [P, 4, P])
        ps_sT = psum("ps_sT", [P, G * P])
        ps_up = psum("ps_up", [P, G, D])
        ps_wts = psum("ps_wts", [P, G, D])
        ps_dst = psum("ps_dst", [P, G, P])
        ps_sum = [psum(f"ps_sum{r}", [P, 2, 2, P]) for r in range(2)]
        ps_msg = psum("ps_msg", [P, G, D])

        cleared = sem("cleared")
        consts = sem("consts")
        loaded = sem("loaded")
        edges_in = sem("edges_in")
        acc_init = [sem(f"acc_init{m}") for m in range(2)]
        dve_pre = sem("dve_pre")
        act_pre = sem("act_pre")
        prepared = sem("prepared")
        weights = sem("weights")
        pool_staged = sem("pool_staged")
        pool_passed = sem("pool_passed")
        gathered = [sem(f"gathered{b}") for b in range(2)]
        basis_staged = sem("basis_staged")
        basisT_ps = sem("basisT_ps")
        senderT_ps = sem("senderT_ps")
        dst_ps = sem("dst_ps")
        basisT_ready = sem("basisT_ready")
        senderT_ready = sem("senderT_ready")
        hid0_ps = sem("hid0_ps")
        hid0_ready = sem("hid0_ready")
        hid1_ps = sem("hid1_ps")
        hid1_ready = sem("hid1_ready")
        up_ps = sem("up_ps")
        wts_ps = sem("wts_ps")
        same_ready = sem("same_ready")
        rows_ready = sem("rows_ready")
        dve_step = sem("dve_step")
        dve_step_dot = sem("dve_step_dot")
        wts_ready = sem("wts_ready")
        mid_ready = sem("mid_ready")
        sum_ps = [sem(f"sum_ps{r}") for r in range(2)]
        sum_ready = [sem(f"sum_ready{r}") for r in range(2)]
        msg_ps = sem("msg_ps")
        msg_ready = sem("msg_ready")
        scattered = [sem(f"scattered{m}") for m in range(2)]
        parts_in = [sem(f"parts_in{b}") for b in range(2)]
        total_ready = sem("total_ready")
        stat_step = sem("stat_step")
        var_ready = sem("var_ready")
        std_ready = sem("std_ready")
        shift_ready = sem("shift_ready")
        normed_ready = sem("normed_ready")
        stored = [sem(f"stored{b}") for b in range(2)]

        block = ctx.enter_context(nc.Block())
        WEIGHT_DMAS = 1 + 3 + G + 2 + 2 + 4 + 1 + 4
        ACC_DMAS = [2, 1 + N * D // (P * ZCOLS)]
        SPANS = [(0, 112), (112, 15)]

        def column(v):
            return v.rearrange("(k a) -> k a", a=1)

        def wide(a, axis, n):
            a = a.unsqueeze(axis)
            shape = list(a.shape)
            shape[axis] = n
            return a.broadcast_to(shape)

        @block.sync
        def _(sp):
            sp.wait_ge(cleared, 5)
            for a, v, w in ((src_all, src, 1), (dst_int, dst, 1), (len_all, edge_len, 1), (vec_all, edge_vec, 3)):
                flat = v if w == 1 else v.rearrange("e c -> (e c)")
                to = a if w == 1 else a[:, :, :].rearrange("p t c -> p (t c)")
                for p0, n in SPANS:
                    sp.dma_start(to[p0:p0 + n, 0:PITCH * w],
                                 flat[p0 * PITCH * w:(p0 + n) * PITCH * w].rearrange("(p t) -> p t", p=n)
                                 ).then_inc(edges_in, 16)
                sp.dma_start(to[P - 1:P, 0:LAST * w],
                             flat[(P - 1) * PITCH * w:E * w].rearrange("(p t) -> p t", p=1)).then_inc(edges_in, 16)
            sp.wait_ge(consts, 1)
            sp.dma_start(up_raw[0:MUL, 0:MUL], W_up0).then_inc(loaded, 16)
            for c in range(3):
                rows = up_raw[MUL + c:MUL + c + 3 * (MUL - 1) + 1:3, MUL * (c + 1):MUL * (c + 2)]
                sp.dma_start(rows, W_up1).then_inc(loaded, 16)
            for i in range(G):
                sp.dma_start(mlp0[NB * i:NB * (i + 1), i // 2, HID * (i % 2):HID * (i % 2 + 1)], w0
                             ).then_inc(loaded, 16)
            for s in range(2):
                half = slice(HID * s, HID * (s + 1))
                sp.dma_start(mlp1[half, half], w1).then_inc(loaded, 16)
                sp.dma_start(mlp2[half, s, :], w2).then_inc(loaded, 16)
                sp.dma_start(bias0[half, :], column(b0)).then_inc(loaded, 16)
                sp.dma_start(bias1[half, :], column(b1)).then_inc(loaded, 16)
            sp.dma_start(bias2[:, :], b2.partition_broadcast(P)).then_inc(loaded, 16)
            for h in range(2):
                for k in range(2):
                    w = W_out0 if h == 0 and k == 0 else W_out1
                    sp.dma_start(out_raw[2 * MUL * k:2 * MUL * (k + 1), h, MUL * k:MUL * (k + 1)], w
                                 ).then_inc(loaded, 16)
            sp.wait_ge(cleared, 6)
            for m in range(2):
                sp.dma_start(acc[m][N:N + P, :], zeros[:, 0:D]).then_inc(acc_init[m], 16)
            for k in range(N * D // (P * ZCOLS)):
                rows = acc[1][0:N, :].rearrange("n d -> (n d)")[k * P * ZCOLS:(k + 1) * P * ZCOLS]
                sp.dma_start(rows.rearrange("(p f) -> p f", p=P), zeros[:, :]).then_inc(acc_init[1], 16)
            sp.dma_start(acc[0][0:N, :].rearrange("n d -> (n d)").rearrange("(p f) -> p f", p=P),
                         x.rearrange("n d -> (n d)").rearrange("(p f) -> p f", p=P)).then_inc(acc_init[0], 16)

            for m in range(2):
                sp.wait_ge(scattered[m], 16 * TILES // 2)

            def load(c, b, first):
                if not first:
                    sp.wait_ge(total_ready, c - 1)
                for part, a in ((part0, acc[0]), (part1, acc[1])):
                    sp.dma_start(part[:, b, :, :].rearrange("p r d -> p (r d)"),
                                 a[bass.ds(c * CHUNK, CHUNK), :].rearrange("(p r) d -> p (r d)", p=P)
                                 ).then_inc(parts_in[b], 16)

            def store(c, b):
                sp.wait_ge(normed_ready, c + 1)
                sp.dma_start(out[bass.ds(c * CHUNK, CHUNK), :].rearrange("(p r) d -> p (r d)", p=P),
                             normed[:, b, :, :].rearrange("p r d -> p (r d)")).then_inc(stored[b], 16)

            load(0, 0, True)
            load(1, 1, True)
            with sp.Fori(0, CHUNKS // 2 - 1) as i:
                for b in range(2):
                    load(2 * i + 2 + b, b, False)
                    store(2 * i + b, b)
            sp.wait_ge(total_ready, CHUNKS - 1)
            for part, a in ((part0, acc[0]), (part1, acc[1])):
                sp.dma_start(part[0:REST, 0, 0, :], a[CHUNKS * CHUNK:N, :]).then_inc(parts_in[0], 16)
            for b in range(2):
                store(CHUNKS - 2 + b, b)
            sp.wait_ge(normed_ready, CHUNKS + 1)
            sp.dma_start(out[CHUNKS * CHUNK:N, :], normed[0:REST, 0, 0, :]).then_inc(stored[0], 16)
            sp.wait_ge(stored[0], 16 * (CHUNKS // 2 + 1))
            sp.wait_ge(stored[1], 16 * (CHUNKS // 2))

        @block.gpsimd
        def _(pool):
            pool.memset(src_all[:, :], 0).then_inc(cleared, 1)
            pool.iota(dump_row[:, :], [[0, TILES]], base=N, channel_multiplier=1).then_inc(cleared, 1)
            pool.memset(len_all[:, :], 0.0).then_inc(cleared, 1)
            pool.memset(vec_all[:, :, :], 0.0).then_inc(cleared, 1)
            pool.wait_ge(cleared, 4)
            pool.tensor_copy(dst_int[:, :], dump_row[:, :]).then_inc(cleared, 1)
            for a in (up_raw[:, :], mlp0[:, :, :], mlp1[:, :], mlp2[:, :, :]):
                pool.memset(a, 0.0)
            pool.memset(out_raw[:, :, :], 0.0).then_inc(consts, 1)
            for k in range(NB):
                pool.memset(centers[:, k:k + 1], k / (NB - 1))
            pool.memset(ident[:, :], 0.0)
            pool.memset(eps[:, :], EPS)
            pool.memset(earlier[:, :], 1.0).then_inc(consts, 1)
            pool.memset(zeros[:, :], 0.0).then_inc(cleared, 1)
            pool.wait_ge(consts, 2)
            pool.affine_select(out=ident[:, :], in_=ident[:, :], compare_op=ALU.not_equal, fill=1.0,
                               base=0, pattern=[[-1, P]], channel_multiplier=1).then_inc(consts, 1)
            pool.affine_select(out=earlier[:, :], in_=earlier[:, :], compare_op=ALU.is_gt, fill=0.0,
                               base=0, pattern=[[-1, P]], channel_multiplier=1).then_inc(consts, 1)
            pool.wait_ge(edges_in, 16 * 12)

            def gather(u, b, first):
                if not first:
                    pool.wait_ge(senderT_ps, u - 1)
                    pool.sem_inc(pool_passed, 1)
                for i in range(G):
                    pool.indirect_dma_start(sender[:, b, i, :], None, x,
                                            bass.IndirectOffsetOnAxis(ap=src_now[:, b, i:i + 1], axis=0)
                                            ).then_inc(gathered[b], 16)
                    yield

            def scatter(v, b, first):
                pool.wait_ge(msg_ready, v + 1)
                for i in range(G):
                    m = i % 2
                    if first and i < 2:
                        pool.wait_ge(acc_init[m], 16 * ACC_DMAS[m])
                    else:
                        pool.wait_ge(scattered[m], v * (16 * G // 2) + 16 * (i // 2))
                        pool.sem_inc(pool_passed, 1)
                    pool.indirect_dma_start(acc[m], bass.IndirectOffsetOnAxis(ap=row_now[:, b, i:i + 1], axis=0),
                                            msg[:, b, i, :], None, compute_op=ALU.add).then_inc(scattered[m], 16)
                    yield

            def stage(s, to_gather, to_scatter, k):
                if to_gather:
                    b = k % 2
                    if k >= 2:
                        pool.wait_ge(gathered[b], s * (16 * G // 2) - 16 * G * b // 2)
                    pool.tensor_copy(src_now[:, b, :], src_all[:, bass.ds(s * G, G)]).then_inc(pool_staged, 1)
                if to_scatter:
                    v, b = s - LAG, (k - LAG) % 2
                    pool.wait_ge(rows_ready, v + 1)
                    pool.tensor_copy(row_now[:, b, :], row_all[:, bass.ds(v * G, G)]).then_inc(pool_staged, 1)

            def step(s, k, staged, to_gather=True, to_scatter=True):
                stage(s, to_gather, to_scatter, k)
                pool.wait_ge(pool_staged, staged)
                g = gather(s, k % 2, k < 2) if to_gather else iter(())
                c = scatter(s - LAG, (k - LAG) % 2, k == LAG) if to_scatter else iter(())
                for _ in range(G):
                    next(g, None)
                    next(c, None)

            for s in range(4):
                step(s, s, s + 1 + max(0, s + 1 - LAG), True, s >= LAG)
            with pool.Fori(2, UNITS // 2) as j:
                for k in range(2):
                    step(2 * j + k, 4 + k, 4 * j + 2 * k + 2 - LAG)
            for s in range(UNITS, UNITS + LAG):
                step(s, s, s + 1 - LAG + UNITS, False, True)

            def add(c, k, rows=ROWS, parts=P):
                b = k % 2
                pool.wait_ge(parts_in[b], c * 16 + 32 - 16 * b)
                if k >= 2:
                    pool.wait_ge(normed_ready, c - 1)
                pool.tensor_tensor(total[0:parts, b, 0:rows, :], part0[0:parts, b, 0:rows, :],
                                   part1[0:parts, b, 0:rows, :], ALU.add).then_inc(total_ready, 1)

            for c in range(2):
                add(c, c)
            with pool.Fori(1, CHUNKS // 2) as j:
                for k in range(2):
                    add(2 * j + k, 2 + k)
            add(CHUNKS, CHUNKS, 1, REST)

        @block.tensor
        def _(pe):
            pe.wait_ge(consts, 4)
            pe.wait_ge(weights, 5)
            pe.wait_ge(loaded, 16 * WEIGHT_DMAS)

            def turn(u, k):
                b = k % 2
                pe.wait_ge(basis_staged, u + 1)
                if k >= 1:
                    pe.wait_ge(hid1_ready, u)
                pe.transpose(ps_hid[0:G * NB, 2, :], basis[:, b, :], ident[:, :]).then_inc(basisT_ps, 1)
                if k >= 1:
                    pe.wait_ge(same_ready, u)
                for i in range(G):
                    mm = pe.transpose(ps_dst[:, i, :], dst_now[:, b, i:i + 1].broadcast_to([P, P]), ident[:, :])
                mm.then_inc(dst_ps, 1)
                pe.wait_ge(gathered[b], u * (16 * G // 2) + 16 * G - 16 * G * b // 2)
                if k >= 1:
                    pe.wait_ge(senderT_ready, u)
                for i in range(G):
                    mm = pe.transpose(ps_sT[:, P * i:P * (i + 1)], sender[:, b, i, :], ident[:, :])
                mm.then_inc(senderT_ps, 1)

            def hidden0(u, k):
                b = k % 2
                pe.wait_ge(basisT_ready, u + 1)
                for q in range(2):
                    mm = pe.matmul(ps_hid[:, q, :], mlp0[:, q, :], basisT[:, b, :], start=True, stop=True)
                mm.then_inc(hid0_ps, 1)

            def hidden1(u, k):
                pe.wait_ge(hid0_ready, u + 1)
                pe.matmul(ps_hid[:, 2:4, :], mlp1[:, :], hid0[:, k % 2, :], start=True, stop=True
                          ).then_inc(hid1_ps, 1)

            def project_up(u, k):
                b = k % 2
                pe.wait_ge(senderT_ready, u + 1)
                if k >= 1:
                    pe.wait_ge(mid_ready, u)
                for i in range(G):
                    mm = pe.matmul(ps_up[:, i, :], senderT[:, b, P * i:P * (i + 1)], up[:, :], start=True, stop=True)
                mm.then_inc(up_ps, 1)

            def radial(u, k):
                b = k % 2
                pe.wait_ge(hid1_ready, u + 1)
                for i in range(G):
                    mm = pe.matmul(ps_wts[:, i, :], hid1[:, b, P * (i // 2):P * (i // 2 + 1)], mlp2[:, i % 2, :],
                                   start=True, stop=True)
                mm.then_inc(wts_ps, 1)

            def sums(v, k, r):
                b = k % 2
                if r == 0:
                    pe.wait_ge(mid_ready, v + 1)
                if k >= 1:
                    pe.wait_ge(sum_ready[r], v)
                for i in range(2):
                    for h in range(2):
                        mm = pe.matmul(ps_sum[r][:, i, h, :], mid[:, b, 2 * r + i, P * h:P * (h + 1)],
                                       same[:, b, 2 * r + i, :], start=True, stop=True)
                mm.then_inc(sum_ps[r], 1)

            def project_out(v, k):
                b = k % 2
                if k >= 1:
                    pe.wait_ge(msg_ready, v)
                for i in range(G):
                    if i % 2 == 0:
                        pe.wait_ge(sum_ready[i // 2], v + 1)
                    for h in range(2):
                        mm = pe.matmul(ps_msg[:, i, 2 * MUL * h:2 * MUL * (h + 1)], sumT[:, b, i, h, :],
                                       outw[:, h, :], start=True, stop=True)
                mm.then_inc(msg_ps, 1)

            def unit(u, k, tail=False):
                if not tail:
                    turn(u, k)
                    hidden0(u, k)
                if k >= 1:
                    sums(u - 1, k - 1, 0)
                if not tail:
                    hidden1(u, k)
                if k >= 1:
                    sums(u - 1, k - 1, 1)
                    project_out(u - 1, k - 1)
                if not tail:
                    project_up(u, k)
                    radial(u, k)

            for u in range(2):
                unit(u, u)
            with pe.Fori(1, UNITS // 2) as j:
                for k in range(2):
                    unit(2 * j + k, 4 + k)
            unit(UNITS, UNITS, tail=True)

        @block.scalar
        def _(act):
            act.wait_ge(dve_pre, 1)
            act.activation(norm[:, :], norm[:, :], ACT.Sqrt).then_inc(act_pre, 1)
            act.wait_ge(dve_pre, 4)
            act.activation(basis_all[:, :, :], basis_all[:, :, :], ACT.Square, scale=float(NB - 1)
                           ).then_inc(act_pre, 1)
            act.wait_ge(act_pre, 2)
            act.activation(basis_all[:, :, :], basis_all[:, :, :], ACT.Exp, scale=-0.5).then_inc(act_pre, 1)
            act.wait_ge(loaded, 16 * WEIGHT_DMAS)
            act.mul(up[:, :], up_raw[:, :], MUL ** -0.5).then_inc(weights, 1)
            by = 1.0 / (AVG * (2 * MUL) ** 0.5)
            for k in range(4):
                for h in range(2):
                    rows = slice(MUL * k, MUL * (k + 1))
                    y = 3 ** 0.5 if k == 2 or (k == 0 and h == 1) else 1.0
                    mm = act.mul(outw[rows, h, :], out_raw[rows, h, :], by * y)
                mm.then_inc(weights, 1)

            def stage(u, k):
                b = k % 2
                act.copy(basis[:, b, :].rearrange("p (i k) -> p i k", k=NB), basis_all[:, bass.ds(u * G, G), :])
                act.copy(dst_now[:, b, :], dst_all[:, bass.ds(u * G, G)]).then_inc(basis_staged, 1)

            def sums_out(v, k, r):
                b = k % 2
                act.wait_ge(sum_ps[r], v + 1)
                act.copy(sumT[:, b, 2 * r:2 * r + 2, :, :], ps_sum[r][:, :, :, :]).then_inc(sum_ready[r], 1)

            def msg_out(v, k):
                b = k % 2
                act.wait_ge(msg_ps, v + 1)
                if k >= 2:
                    for m in range(2):
                        act.wait_ge(scattered[m], v * (16 * G // 2) - 16 * G // 2)
                act.copy(msg[:, b, :, 0:MUL], ps_msg[:, :, 0:MUL])
                act.copy(msg[:, b, :, MUL:D].rearrange("p i (k c) -> p i c k", c=3),
                         ps_msg[:, :, MUL:D].rearrange("p i (c k) -> p i c k", c=3)).then_inc(msg_ready, 1)

            def unit(u, k, tail=False, last=False):
                b = k % 2
                if not tail:
                    act.wait_ge(basisT_ps, u + 1)
                    act.copy(basisT[:, b, :], ps_hid[0:G * NB, 2, :]).then_inc(basisT_ready, 1)
                    act.wait_ge(senderT_ps, u + 1)
                    act.copy(senderT[:, b, :], ps_sT[:, :]).then_inc(senderT_ready, 1)
                    if not last:
                        stage(u + 2, k)
                    act.wait_ge(hid0_ps, u + 1)
                    act.activation(hid0[:, b, :], ps_hid[:, 0:2, :].rearrange("p q e -> p (q e)"), ACT.Silu,
                                   bias=bias0[:, :]).then_inc(hid0_ready, 1)
                if k >= 1:
                    sums_out(u - 1, k - 1, 0)
                if not tail:
                    act.wait_ge(hid1_ps, u + 1)
                    act.activation(hid1[:, b, :], ps_hid[:, 2:4, :].rearrange("p q e -> p (q e)"), ACT.Silu,
                                   bias=bias1[:, :]).then_inc(hid1_ready, 1)
                if k >= 1:
                    sums_out(u - 1, k - 1, 1)
                    msg_out(u - 1, k - 1)

            act.wait_ge(prepared, 3)
            stage(0, 0)
            stage(1, 1)
            for u in range(2):
                unit(u, u)
            with act.Fori(1, UNITS // 2 - 1) as j:
                for k in range(2):
                    unit(2 * j + k, 4 + k)
            for u in range(UNITS - 2, UNITS):
                unit(u, u, last=True)
            unit(UNITS, UNITS, tail=True)

            def normalise(c, k, rows=ROWS, parts=P):
                b = k % 2
                act.wait_ge(var_ready, c + 1)
                act.activation(std[0:parts, b, 0:rows], var[0:parts, b, 0:rows], ACT.Sqrt, bias=eps[0:parts, :]
                               ).then_inc(std_ready, 1)
                act.wait_ge(shift_ready, c + 1)
                if k >= 2:
                    act.wait_ge(stored[b], c * 8 - 8 * b)
                for r in range(rows):
                    mm = act.activation(normed[0:parts, b, r, :], total[0:parts, b, r, :], ACT.Identity,
                                        scale=rstd[0:parts, b, r:r + 1], bias=shift[0:parts, b, r:r + 1])
                mm.then_inc(normed_ready, 1)

            for c in range(2):
                normalise(c, c)
            with act.Fori(1, CHUNKS // 2) as j:
                for k in range(2):
                    normalise(2 * j + k, 2 + k)
            normalise(CHUNKS, CHUNKS, 1, REST)

        @block.vector
        def _(dve):
            dve.wait_ge(edges_in, 16 * 12)
            dve.wait_ge(consts, 4)
            dve.tensor_tensor(vec_sq[:, :, :], vec_all[:, :, :], vec_all[:, :, :], ALU.mult).then_inc(prepared, 1)
            dve.wait_ge(prepared, 1)
            dve.tensor_reduce(norm[:, :], vec_sq[:, :, :], AX_X, ALU.add).then_inc(dve_pre, 1)
            dve.tensor_copy(dump_rowf[:, :], dump_row[:, 0:G]).then_inc(dve_pre, 1)
            dve.tensor_scalar(len_clip[:, :], len_all[:, :], 0.0, 1.0, ALU.max, ALU.min).then_inc(dve_pre, 1)
            dve.wait_ge(dve_pre, 3)
            dve.tensor_tensor(basis_all[:, :, :], wide(len_clip[:, :], 2, NB), wide(centers[:, :], 1, TILES),
                              ALU.subtract).then_inc(dve_pre, 1)
            dve.tensor_scalar(len_all[:, :], len_all[:, :], 1.0, NB ** 0.5, ALU.is_le, ALU.mult).then_inc(dve_pre, 1)
            dve.tensor_copy(dst_all[:, :], dst_int[:, :]).then_inc(prepared, 1)
            dve.wait_ge(act_pre, 1)
            dve.tensor_scalar(norm[:, :], norm[:, :], 1e-12, None, ALU.add).then_inc(dve_pre, 1)
            dve.wait_ge(dve_pre, 6)
            dve.reciprocal(norm[:, :], norm[:, :]).then_inc(dve_pre, 1)
            dve.wait_ge(dve_pre, 7)
            dve.tensor_tensor(vec_all[:, :, :], vec_all[:, :, :], wide(norm[:, :], 2, 3), ALU.mult
                              ).then_inc(dve_pre, 1)
            dve.wait_ge(act_pre, 3)
            dve.tensor_tensor(basis_all[:, :, :], basis_all[:, :, :], wide(len_all[:, :], 2, NB), ALU.mult
                              ).then_inc(prepared, 1)
            dve.wait_ge(dve_pre, 8)
            dve.wait_ge(loaded, 16 * WEIGHT_DMAS)

            def equal_receivers(u, k):
                b = k % 2
                dst_col = dst_all[:, bass.ds(u * G, G)]
                dve.wait_ge(dst_ps, u + 1)
                if k >= 2:
                    dve.wait_ge(sum_ps[1], u - 1)
                dve.tensor_tensor(same[:, b, :, :], ps_dst[:, :, :], wide(dst_col, 2, P), ALU.is_equal
                                  ).then_inc(same_ready, 1)
                dve.wait_ge(same_ready, u + 1)
                for i in range(G):
                    mm = dve.tensor_tensor_reduce(junk[:, b, i, :], same[:, b, i, :], earlier[:, :], 1.0, 0.0,
                                                  ALU.mult, ALU.add, count[:, b, i:i + 1])
                mm.then_inc(dve_step, 1)
                dve.tensor_tensor(rowf[:, b, :], dump_rowf[:, :], dst_col, ALU.subtract).then_inc(dve_step, 1)
                dve.wait_ge(dve_step, 5 * u + 2)
                dve.scalar_tensor_tensor(out=rowf[:, b, :], in0=count[:, b, :], scalar=1.0, in1=rowf[:, b, :],
                                         op0=ALU.min, op1=ALU.mult).then_inc(dve_step, 1)
                dve.wait_ge(dve_step, 5 * u + 3)
                dve.tensor_tensor(row_all[:, bass.ds(u * G, G)], rowf[:, b, :], dst_col, ALU.add
                                  ).then_inc(rows_ready, 1)

            def products(u, k):
                b = k % 2
                y = vec_all[:, bass.ds(u * G, G), :]
                w, md = wts[:, b, :, :], mid[:, b, :, :]
                s, v = ps_up[:, :, 0:MUL], ps_up[:, :, MUL:D].rearrange("p i (c k) -> p i c k", c=3)
                pairs = md[:, :, 0:8 * MUL].rearrange("p i (c k) -> p i c k", c=4)
                pj = proj[:, b, :, :].rearrange("p i (c k) -> p i c k", c=3)
                dve.wait_ge(wts_ps, u + 1)
                dve.tensor_tensor(w, ps_wts[:, :, :], wide(bias2[:, :], 1, G), ALU.add).then_inc(wts_ready, 1)
                dve.wait_ge(up_ps, u + 1)
                dve.tensor_tensor(pj, v, wide(y, 3, MUL), ALU.mult).then_inc(dve_step, 1)
                dve.wait_ge(wts_ready, u + 1)
                dve.tensor_tensor(md[:, :, 0:MUL], w[:, :, 0:MUL], s, ALU.mult)
                dve.tensor_tensor(md[:, :, 8 * MUL:9 * MUL], w[:, :, MUL:2 * MUL], s, ALU.mult
                                  ).then_inc(dve_step, 1)
                dve.tensor_tensor(pairs[:, :, 1:4, MUL:2 * MUL], v, wide(w[:, :, 2 * MUL:3 * MUL], 2, 3), ALU.mult)
                dve.wait_ge(dve_step, 5 * u + 5)
                dve.tensor_reduce(dot[:, b, :, :], pj.rearrange("p i c k -> p i k c"), AX_X, ALU.add
                                  ).then_inc(dve_step_dot, 1)
                dve.tensor_tensor(pairs[:, :, 1:4, 0:MUL], wide(md[:, :, 8 * MUL:9 * MUL], 2, 3), wide(y, 3, MUL),
                                  ALU.mult)
                dve.wait_ge(dve_step_dot, u + 1)
                dve.tensor_tensor(md[:, :, MUL:2 * MUL], w[:, :, 3 * MUL:D], dot[:, b, :, :], ALU.mult
                                  ).then_inc(mid_ready, 1)

            def unit(u, k):
                equal_receivers(u, k)
                products(u, k)

            for u in range(2):
                unit(u, u)
            with dve.Fori(1, UNITS // 2) as j:
                for k in range(2):
                    unit(2 * j + k, 4 + k)

            def statistics(c, k, rows=ROWS, parts=P):
                b = k % 2
                dve.wait_ge(total_ready, c + 1)
                for r in range(rows):
                    mm = dve.bn_stats(stats[0:parts, b, r, :], total[0:parts, b, r, :])
                mm.then_inc(stat_step, 1)
                st = stats[0:parts, b, 0:rows, :]
                mn, hg, gs = (a[0:parts, b, 0:rows] for a in (mean, half_gap, gap_sq))
                vr, sd, rs, sh = (a[0:parts, b, 0:rows] for a in (var, std, rstd, shift))
                dve.wait_ge(stat_step, 5 * c + 1)
                dve.tensor_tensor(mn, st[:, :, 1], st[:, :, 4], ALU.add)
                dve.tensor_tensor(vr, st[:, :, 2], st[:, :, 5], ALU.add)
                dve.tensor_tensor(hg, st[:, :, 1], st[:, :, 4], ALU.subtract).then_inc(stat_step, 1)
                dve.wait_ge(stat_step, 5 * c + 2)
                dve.tensor_scalar(mn, mn, 0.5, None, ALU.mult)
                dve.scalar_tensor_tensor(out=gs, in0=hg, scalar=0.25, in1=hg, op0=ALU.mult, op1=ALU.mult
                                         ).then_inc(stat_step, 1)
                dve.wait_ge(stat_step, 5 * c + 3)
                dve.scalar_tensor_tensor(out=vr, in0=vr, scalar=1.0 / D, in1=gs, op0=ALU.mult, op1=ALU.add
                                         ).then_inc(var_ready, 1)
                dve.wait_ge(std_ready, c + 1)
                if k >= 2:
                    dve.wait_ge(normed_ready, c - 1)
                dve.reciprocal(rs, sd).then_inc(stat_step, 1)
                dve.wait_ge(stat_step, 5 * c + 4)
                dve.scalar_tensor_tensor(out=sh, in0=mn, scalar=-1.0, in1=rs, op0=ALU.mult, op1=ALU.mult
                                         ).then_inc(shift_ready, 1)
                dve.nop().then_inc(stat_step, 1)

            for c in range(2):
                statistics(c, c)
            with dve.Fori(1, CHUNKS // 2) as j:
                for k in range(2):
                    statistics(2 * j + k, 2 + k)
            statistics(CHUNKS, CHUNKS, 1, REST)


_INS = ['x', 'src', 'dst', 'edge_attr_3', 'edge_weight', 'L0_gnn_W_up0', 'L0_gnn_W_up1', 'L0_gnn_mlp_w0',
        'L0_gnn_mlp_b0', 'L0_gnn_mlp_w1', 'L0_gnn_mlp_b1', 'L0_gnn_mlp_w2', 'L0_gnn_mlp_b2', 'L0_gnn_W_out0',
        'L0_gnn_W_out1']


def kernel(**inputs):
    import numpy as _np
    import concourse.bacc as _bacc
    from concourse import mybir as _mybir
    from concourse.bass_utils import run_bass_kernel_spmd as _run

    nc = _bacc.Bacc("TRN2", target_bir_lowering=False, num_devices=1)
    arrays, args = {}, []
    for name in _INS:
        a = _np.ascontiguousarray(inputs[name])
        arrays[f"in_{name}_dram"] = a
        args.append(nc.dram_tensor(f"in_{name}_dram", a.shape, _mybir.dt.from_np(a.dtype), kind="ExternalInput").ap())
    args.append(nc.dram_tensor("out_0_dram", (N, D), F32, kind="ExternalOutput").ap())
    bass_gnn(nc, *args)
    r = _run(nc, [arrays], core_ids=[0])
    return r.results[0]["out_0_dram"]
```

```python
from contextlib import ExitStack

import concourse.bass as bass
from concourse import mybir
from concourse.alu_op_type import AluOpType as ALU

F32 = mybir.dt.float32
I32 = mybir.dt.int32
ACT = mybir.ActivationFunctionType
AX_X = mybir.AxisListType.X

P = 128
N = 50000
E = 50000
D = 128
MUL = 32
NB = 8
HID = 64
AVG = 16.0
EPS = 1e-5

G = 4
ROWE = G * P
UNITS = -(-E // ROWE)
FULL = E // ROWE
TILES = UNITS * G
PAIRS = UNITS // 2
LAG = 6
RING = 4
STATS_AFTER = 5
NORM_AFTER = STATS_AFTER + 1
RATE = 2 / 3
FAR = 100.0
PRE = 7
DENSE_FROM = 4
SPARE = 3 * P
MIDW = 9 * MUL

ROWS = 13
CHUNK = P * ROWS
CHUNKS = N // CHUNK
REST = N - CHUNKS * CHUNK
PIECE = 2500
PIECES = N // PIECE
ROUNDS = 3
SSTEPS = 5 + 3 * ROUNDS
RSQRT_BITS = float(0x5f3759df)
assert UNITS % 2 == 0 and LAG % 2 == 0 and UNITS <= P and FULL == UNITS - 1 and FULL >= 96
assert NORM_AFTER > STATS_AFTER and NORM_AFTER > RING // 2 and (UNITS - 2) % RING == 0 and CHUNKS % 2 == 0 and PIECES % 2 == 0 and N % PIECE == 0 and REST <= P


def bass_gnn(nc, x, src, dst, edge_vec, edge_len, W_up0, W_up1, w0, b0, w1, b1, w2, b2, W_out0, W_out1, out):
    acc = nc.dram_tensor("acc", (N + SPARE, D), F32, kind="Internal").ap()

    ctx = ExitStack()
    with ctx:
        def sb(name, shape, dt=F32):
            return ctx.enter_context(nc.sbuf_tensor(name, shape, dt))

        def psum(name, shape):
            return ctx.enter_context(nc.psum_tensor(name, shape, F32))

        def sem(name):
            return ctx.enter_context(nc.semaphore(name))

        ident = sb("ident", [P, P])
        backward = sb("backward", [P, P])
        earlier = sb("earlier", [P, P])
        dump_row = sb("dump_row", [P, 2], I32)
        dump_rowf = sb("dump_rowf", [P, 2])
        zeros = sb("zeros", [P, SPARE // P, D])
        minus_k = sb("minus_k", [P, NB])
        up_raw = sb("up_raw", [P, D])
        up = sb("up", [P, D])
        mlp0_raw = sb("mlp0_raw", [G * NB, 2, 2 * HID])
        mlp0 = sb("mlp0", [G * NB, 2, 2 * HID])
        mlp1 = sb("mlp1", [2 * HID, 2 * HID])
        mlp2 = sb("mlp2", [2 * HID, 2, D])
        start = sb("start", [HID, 2])
        bias0 = sb("bias0", [2 * HID, 1])
        bias1 = sb("bias1", [2 * HID, 1])
        bias2 = sb("bias2", [P, D])
        out_raw = sb("out_raw", [P, 2, 2 * MUL])
        outw = sb("outw", [P, 2, 2 * MUL])
        src_raw = sb("src_raw", [UNITS, G, P], I32)
        dst_raw = sb("dst_raw", [UNITS, G, P], I32)
        src_rawf = sb("src_rawf", [UNITS, G, P])
        dst_rawf = sb("dst_rawf", [UNITS, G, P])
        len_raw = sb("len_raw", [UNITS, G, P])
        vec_raw = sb("vec_raw", [UNITS, G, P, 3])
        low_raw = sb("low_raw", [UNITS, G])
        high_raw = sb("high_raw", [UNITS, G])
        low = sb("low", [1, UNITS, G])
        high = sb("high", [1, UNITS, G])
        meet = sb("meet", [1, TILES])
        meet_too = sb("meet_too", [1, TILES])
        piece_int = sb("piece_int", [1, UNITS], I32)
        pieces = sb("pieces", [1, UNITS])
        meet_unit = sb("meet_unit", [1, UNITS])
        by_index = sb("by_index", [1, PAIRS])
        orders = sb("orders", [1, UNITS])
        scatter_orders = sb("scatter_orders", [1, UNITS], I32)
        least = [sb(f"least{k}", [1, 2 * P]) for k in range(2)]
        final_int = sb("final_int", [1, PAIRS], I32)
        rising = sb("rising", [1, PAIRS])
        final = sb("final", [1, 1 + PAIRS])
        fresh = sb("fresh", [1, PAIRS])
        half_chunk = sb("half_chunk", [1, PAIRS])
        dense_orders = sb("dense_orders", [1, NORM_AFTER + PAIRS], I32)
        done_count = sb("done_count", [1, 3], I32)
        dst_all = sb("dst_all", [P, UNITS, G])
        gap_all = sb("gap_all", [P, UNITS, G])
        index = sb("index", [P, UNITS + LAG, 2, G], I32)
        vec_all = sb("vec_all", [P, TILES, 3])
        vec_sq = sb("vec_sq", [P, TILES, 3])
        norm = sb("norm", [P, TILES])
        len_all = sb("len_all", [P, TILES])
        beyond = sb("beyond", [P, TILES])
        len_clip = sb("len_clip", [P, TILES])
        basis_all = sb("basis_all", [P, TILES, NB])
        index_now = sb("index_now", [P, 2, 2, G], I32)
        sender = sb("sender", [P, RING, G, D])
        basis = sb("basis", [P, 2, G * NB])
        dst_now = sb("dst_now", [P, 2, G])
        basisT = sb("basisT", [G * NB, 2, P])
        senderT = sb("senderT", [P, 2, G * P])
        hid0 = sb("hid0", [2 * HID, 2, 2 * P])
        hid1 = sb("hid1", [2 * HID, 2, 2 * P])
        same = sb("same", [P, 2, G, P])
        junk = sb("junk", [P, 2, G, P])
        count = sb("count", [P, 2, G])
        rowf = sb("rowf", [P, 2, G])
        wts = sb("wts", [P, 2, G, D])
        mid = sb("mid", [P, 2, G, MIDW])
        proj = sb("proj", [P, 2, G, 3 * MUL])
        dot = sb("dot", [P, 2, G, MUL])
        sumT = sb("sumT", [P, 2, G, 2, P])
        msg = sb("msg", [P, RING, G, D])
        total = sb("total", [P, 4, ROWS, D])
        normed = sb("normed", [P, 2, ROWS, D])
        stats = sb("stats", [P, ROWS, 6])
        mean = sb("mean", [P, ROWS])
        half_gap = sb("half_gap", [P, ROWS])
        gap_sq = sb("gap_sq", [P, ROWS])
        var = sb("var", [P, ROWS])
        bits = sb("bits", [P, ROWS], I32)
        rstd = sb("rstd", [P, 2, ROWS])
        shift = sb("shift", [P, 2, ROWS])

        ps_hid = psum("ps_hid", [P, 4, P])
        ps_sT = psum("ps_sT", [P, G * P])
        ps_up = psum("ps_up", [P, G, D])
        ps_wts = psum("ps_wts", [P, G, D])
        ps_dst = psum("ps_dst", [P, G, P])
        ps_sum = [psum(f"ps_sum{r}", [P, 2, 2, P]) for r in range(2)]
        ps_msg = psum("ps_msg", [P, G, D])

        ps_src, ps_len, ps_low, ps_high = ps_sT[:, :].rearrange("p (i e) -> p i e", i=G), ps_wts, ps_msg, ps_hid
        ps_vec = [ps_up] + [a[:, :, :, :].rearrange("p i h e -> p (i h) e") for a in ps_sum]

        cleared = sem("cleared")
        consts = sem("consts")
        loaded = sem("loaded")
        edges_in = sem("edges_in")
        edges_f32 = sem("edges_f32")
        tile_ends = sem("tile_ends")
        planes = sem("planes")
        ends_ps = sem("ends_ps")
        act_planes = sem("act_planes")
        acc_init = [sem(f"acc_init{b}") for b in range(2)]
        spare_rows = sem("spare_rows")
        table_step = sem("table_step")
        tables = sem("tables")
        dve_pre = sem("dve_pre")
        act_pre = sem("act_pre")
        dump_ready = sem("dump_ready")
        prepared = sem("prepared")
        directions_ready = sem("directions_ready")
        weights = sem("weights")
        zeroed = sem("zeroed")
        index_in = sem("index_in")
        pool_staged = sem("pool_staged")
        pool_passed = sem("pool_passed")
        sp_passed = sem("sp_passed")
        gathered = [sem(f"gathered{b}") for b in range(2)]
        basis_staged = sem("basis_staged")
        basisT_ps = sem("basisT_ps")
        senderT_ps = sem("senderT_ps")
        dst_ps = sem("dst_ps")
        basisT_ready = sem("basisT_ready")
        senderT_ready = sem("senderT_ready")
        hid0_ps = sem("hid0_ps")
        hid0_ready = sem("hid0_ready")
        hid1_ps = sem("hid1_ps")
        hid1_ready = sem("hid1_ready")
        up_ps = sem("up_ps")
        wts_ps = sem("wts_ps")
        up_used = sem("up_used")
        same_ready = sem("same_ready")
        rows_ready = sem("rows_ready")
        counted = sem("counted")
        rowf_ready = sem("rowf_ready")
        dve_step = sem("dve_step")
        dve_step_dot = sem("dve_step_dot")
        wts_ready = sem("wts_ready")
        mid_ready = sem("mid_ready")
        sum_ps = [sem(f"sum_ps{r}") for r in range(2)]
        sum_ready = [sem(f"sum_ready{r}") for r in range(2)]
        msg_ps = sem("msg_ps")
        msg_ready = sem("msg_ready")
        scattered = [[sem(f"scattered{b}_{i}") for i in range(G)] for b in range(2)]
        total_in = [sem(f"total_in{b}") for b in range(2)]
        stat_step = sem("stat_step")
        shift_ready = sem("shift_ready")
        stats_ready = sem("stats_ready")
        normed_ready = sem("normed_ready")
        stored = [sem(f"stored{b}") for b in range(2)]

        block = ctx.enter_context(nc.Block())
        WEIGHT_DMAS = 1 + 3 + G + 2 + 2 + 4 + 1 + 4
        SPANS = [(0, 4 * G), (4 * G, TILES)]

        def load_edges(engine, arrays):
            for to, v, w in arrays:
                flat = v if w == 1 else v.rearrange("e c -> (e c)")
                rows = to[:, :, :].rearrange("r q p -> r (q p)") if w == 1 else to[:, :, :, :].rearrange("r q p c -> r (q p c)")
                engine.dma_start(rows[0:96, :], flat[0:96 * ROWE * w].rearrange("(r e) -> r e", r=96)
                                 ).then_inc(edges_in, 16)
            engine.wait_ge(cleared, 4)
            for to, v, w in arrays:
                flat = v if w == 1 else v.rearrange("e c -> (e c)")
                rows = to[:, :, :].rearrange("r q p -> r (q p)") if w == 1 else to[:, :, :, :].rearrange("r q p c -> r (q p c)")
                for r0, r1 in ((96, FULL), (FULL, UNITS)):
                    n = (min(E, r1 * ROWE) - r0 * ROWE) * w
                    engine.dma_start(rows[r0:r1, 0:n // (r1 - r0)],
                                     flat[r0 * ROWE * w:r0 * ROWE * w + n].rearrange("(r e) -> r e", r=r1 - r0)
                                     ).then_inc(edges_in, 16)

        def column(v):
            return v.rearrange("(k a) -> k a", a=1)

        def wide(a, axis, n):
            a = a.unsqueeze(axis)
            shape = list(a.shape)
            shape[axis] = n
            return a.broadcast_to(shape)

        def turns(a, w):
            return a.rearrange("p (j w) (q r) -> p w q j r", w=2, r=2)[:, w]

        def row_tiles(a, w):
            return a[:, 2 * w:2 * w + 2, 0:UNITS].rearrange("p q (j r) -> p q j r", r=2)

        @block.sync
        def _(sp):
            load_edges(sp, [(dst_raw, dst, 1), (vec_raw, edge_vec, 3)])
            sp.wait_ge(zeroed, 1)
            sp.dma_start(acc[N:N + SPARE, :].rearrange("(p k) d -> p k d", p=P), zeros[:, :, :]).then_inc(spare_rows, 16)
            def copy(k):
                if k >= 2:
                    sp.wait_ge(acc_init[k % 2], 16 * (k // 2))
                rows = slice(N - (k + 1) * PIECE, N - k * PIECE)
                to, of = (a[rows, :].rearrange("n d -> (n d)").rearrange("(p f) -> p f", p=P) for a in (acc, x))
                sp.dma_start(to, of).then_inc(acc_init[k % 2], 16)

            for k in range(2):
                copy(k)
            sp.wait_ge(consts, 1)
            sp.dma_start(up_raw[0:MUL, 0:MUL], W_up0).then_inc(loaded, 16)
            for c in range(3):
                rows = up_raw[MUL + c:MUL + c + 3 * (MUL - 1) + 1:3, MUL * (c + 1):MUL * (c + 2)]
                sp.dma_start(rows, W_up1).then_inc(loaded, 16)
            for i in range(G):
                sp.dma_start(mlp0_raw[NB * i:NB * (i + 1), i // 2, HID * (i % 2):HID * (i % 2 + 1)], w0
                             ).then_inc(loaded, 16)
            for s in range(2):
                half = slice(HID * s, HID * (s + 1))
                sp.dma_start(mlp1[half, half], w1).then_inc(loaded, 16)
                sp.dma_start(mlp2[half, s, :], w2).then_inc(loaded, 16)
                sp.dma_start(bias0[half, :], column(b0)).then_inc(loaded, 16)
                sp.dma_start(bias1[half, :], column(b1)).then_inc(loaded, 16)
            sp.dma_start(bias2[:, :], b2.partition_broadcast(P)).then_inc(loaded, 16)
            for h in range(2):
                for k in range(2):
                    w = W_out0 if h == 0 and k == 0 else W_out1
                    sp.dma_start(out_raw[2 * MUL * k:2 * MUL * (k + 1), h, MUL * k:MUL * (k + 1)], w
                                 ).then_inc(loaded, 16)
            for k in range(2, PIECES):
                copy(k)
            for b in range(2):
                sp.wait_ge(acc_init[b], 16 * (PIECES // 2))
            sp.wait_ge(tables, 1)

            def load(h, b):
                c = 2 * h + b
                sp.wait_ge(stats_ready, c + 1)
                sp.wait_ge(normed_ready, c + 1)
                sp.dma_start(total[:, bass.ds(2 * (h % 2) + b, 1), :, :].rearrange("p b r d -> p (b r d)"),
                             acc[bass.ds(N - CHUNK - c * CHUNK, CHUNK), :].rearrange("(p r) d -> p (r d)", p=P)
                             ).then_inc(total_in[b], 16)

            def landed(j):
                for b in range(2):
                    for i in range(2, G):
                        sp.wait_ge(scattered[b][i], 16 * j + 16)

            def store(h, b):
                c = 2 * h + b
                sp.wait_ge(normed_ready, c + 5)
                sp.sem_inc(sp_passed, 1)
                sp.dma_start(out[bass.ds(N - CHUNK - c * CHUNK, CHUNK), :].rearrange("(p r) d -> p (r d)", p=P),
                             normed[:, b, :, :].rearrange("p r d -> p (r d)")).then_inc(stored[b], 16)

            def orders_of(at):
                order = sp.value_load(dense_orders[0:1, bass.ds(at, 1)], min_val=0, max_val=2 * CHUNKS - 2)
                return [(order // 4, b, (order // 2 if b else order) % 2) for b in range(2)]

            def pair(j, stores=True):
                if stores:
                    for h, b, now in orders_of(j + 1):
                        with sp.If(now):
                            store(h, b)
                for h, b, now in orders_of(j + NORM_AFTER):
                    with sp.If(now):
                        landed(j)
                        load(h, b)

            with sp.Fori(0, PAIRS - 1) as j:
                pair(j)
            pair(PAIRS - 1, stores=False)
            landed(PAIRS - 1)
            done = sp.value_load(done_count[0:1, 0:1], min_val=0, max_val=CHUNKS - 1)
            with sp.If(done % 2):
                load(done // 2, 1)
            with sp.If(CHUNKS - 1 - done):
                with sp.Fori((done + 1) // 2, CHUNKS // 2) as h:
                    for b in range(2):
                        load(h, b)
            sp.wait_ge(stats_ready, CHUNKS + 1)
            sp.wait_ge(normed_ready, CHUNKS + 1)
            sp.dma_start(total[0:REST, CHUNKS % 4, 0, :], acc[0:REST, :]).then_inc(total_in[0], 16)
            for b in range(2):
                sp.wait_ge(stored[b], 16 * (CHUNKS // 2 + 2 - b))

        @block.gpsimd
        def _(pool):
            pool.memset(src_raw[96:UNITS, :, :], 0).then_inc(cleared, 1)
            pool.iota(dst_raw[96:UNITS, :, :], [[0, G], [1, P]], base=N + 2 * P, channel_multiplier=0).then_inc(cleared, 1)
            pool.memset(len_raw[96:UNITS, :, :], 0.0).then_inc(cleared, 1)
            pool.memset(vec_raw[96:UNITS, :, :, :], 0.0).then_inc(cleared, 1)
            pool.wait_ge(cleared, 4)
            pool.iota(dump_row[:, :], [[P, 2]], base=N, channel_multiplier=1).then_inc(cleared, 1)
            for a in (up_raw[:, :], mlp0_raw[:, :, :], mlp1[:, :], mlp2[:, :, :]):
                pool.memset(a, 0.0)
            pool.memset(out_raw[:, :, :], 0.0).then_inc(consts, 1)
            for k in range(NB):
                pool.memset(minus_k[:, k:k + 1], float(-k))
            pool.memset(ident[:, :], 0.0)
            pool.memset(backward[:, :], 0.0)
            pool.iota(by_index[:, :], [[1, PAIRS]], base=0, channel_multiplier=0,
                      allow_small_or_imprecise_dtypes=True)
            pool.memset(final[:, :], 0.0)
            pool.memset(dense_orders[:, :], 0)
            pool.memset(meet[:, :], 0.0)
            for a in least:
                pool.memset(a[:, :], float(N))
            pool.memset(earlier[:, :], 1.0).then_inc(consts, 1)
            pool.wait_ge(consts, 2)
            pool.affine_select(out=ident[:, :], in_=ident[:, :], compare_op=ALU.not_equal, fill=1.0,
                               base=0, pattern=[[-1, P]], channel_multiplier=1).then_inc(consts, 1)
            pool.affine_select(out=backward[:, :], in_=backward[:, :], compare_op=ALU.not_equal, fill=1.0,
                               base=1 - UNITS, pattern=[[1, P]], channel_multiplier=1).then_inc(consts, 1)
            pool.affine_select(out=earlier[:, :], in_=earlier[:, :], compare_op=ALU.is_gt, fill=0.0,
                               base=0, pattern=[[-1, P]], channel_multiplier=1).then_inc(consts, 1)
            
            def stage(s, b, gathers=True, scatters=True, reused=True):
                if reused:
                    pool.wait_ge(gathered[b], 8 * G * ((min(s, UNITS) if isinstance(s, int) else s) - b))
                if scatters:
                    pool.wait_ge(rows_ready, s - LAG + 1)
                first, last = (0 if gathers else 1), (2 if scatters else 1)
                pool.tensor_copy(index_now[:, b, first:last, :], index[:, bass.ds(s, 1), first:last, :]
                                 .rearrange("p s a i -> p (s a) i")).then_inc(pool_staged, 1)

            def step(s, slot, gathers=True, scatters=True, reused=True, loop=True, following=None):
                v, b, c, msg_slot = s - LAG, slot % 2, (slot + LAG) % 2, (slot - LAG) % RING
                if scatters:
                    order = pool.value_load(scatter_orders[0:1, bass.ds(v, 1)], min_val=4, max_val=4 * PIECES - 1)
                    pool.wait_ge(acc_init[0], 16 * (order // 8) + 16)
                    pool.wait_ge(acc_init[1], 16 * ((order + 4) // 8))
                    meets = [order % 2] + (G - 1) * [(order // 2) % 2]
                pool.wait_ge(pool_staged, s + 1)
                if gathers and reused:
                    pool.wait_ge(senderT_ps, s - RING + 1)
                if scatters:
                    pool.wait_ge(msg_ready, v + 1)
                pool.sem_inc(pool_passed, 1)
                for i in range(G):
                    if gathers:
                        pool.indirect_dma_start(sender[:, slot, i, :], None, x,
                                                bass.IndirectOffsetOnAxis(ap=index_now[:, b, 0, i:i + 1], axis=0)
                                                ).then_inc(gathered[b], 16)
                    if scatters:
                        if i >= 1:
                            before = scattered[c][i - 1], 8 * (v - c) + 16
                        else:
                            before = scattered[1 - c][G - 1], 8 * (v - c) + 16 * c
                        if i >= 2:
                            pool.wait_ge(scattered[c][i - 2], 8 * (v - c) + 16)
                        elif loop:
                            pool.wait_ge(scattered[1 - c][G - 2 + i], 8 * (v - c) + 16 * c)
                        if loop:
                            pool.wait_ge(before[0], before[1] - 16 + 16 * meets[i])
                        elif i >= 1 or s > LAG:
                            pool.wait_ge(*before)
                        pool.sem_inc(pool_passed, 1)
                        pool.indirect_dma_start(acc, bass.IndirectOffsetOnAxis(ap=index_now[:, b, 1, i:i + 1], axis=0),
                                                msg[:, msg_slot, i, :], None, compute_op=ALU.add
                                                ).then_inc(scattered[c][i], 16)
                    if i == 1 and following is not None:
                        stage(s + 1, 1 - b, **following)

            pool.wait_ge(index_in, 1)
            stage(0, 0, scatters=False, reused=False)
            for s in range(LAG):
                step(s, s % RING, scatters=False, reused=s >= RING,
                     following=dict(scatters=s + 1 >= LAG, reused=s + 1 >= 2))
            pool.wait_ge(spare_rows, 16)
            pool.wait_ge(tables, 1)
            rounds = -(-(LAG + 3) // RING), (UNITS - 2) // RING
            for s in range(LAG, rounds[0] * RING):
                step(s, s % RING, loop=s - LAG >= 3, following={})
            with pool.Fori(*rounds) as j:
                for slot in range(RING):
                    step(RING * j + slot, slot, following={})
            for s in range(UNITS - 2, UNITS + LAG):
                step(s, s % RING, gathers=s < UNITS,
                     following=dict(gathers=s + 1 < UNITS) if s + 1 < UNITS + LAG else None)

        @block.tensor
        def _(pe):
            pe.wait_ge(consts, 5)
            pe.wait_ge(edges_f32, 1)
            pe.wait_ge(edges_in, 16 * 12)
            for a, to in ((src_rawf, ps_src), (dst_rawf, ps_dst), (len_raw, ps_len)):
                for q in range(G):
                    mm = pe.transpose(to[:, q, 0:UNITS], a[:, q, :], backward[0:UNITS, 0:UNITS])
                mm.then_inc(planes, 1)
            for c, to in enumerate(ps_vec):
                for q in range(G):
                    mm = pe.transpose(to[:, q, 0:UNITS], vec_raw[:, q, :, c], backward[0:UNITS, 0:UNITS])
                mm.then_inc(planes, 1)
            pe.wait_ge(tile_ends, 2)
            for a, to in ((low_raw, ps_low), (high_raw, ps_high)):
                for q in range(G):
                    mm = pe.transpose(to[0:1, q, 0:UNITS], a[:, q:q + 1], backward[0:UNITS, 0:UNITS])
                mm.then_inc(ends_ps, 1)
            pe.wait_ge(weights, 6)
            pe.wait_ge(act_planes, 4)
            pe.wait_ge(prepared, 3)
            pe.wait_ge(index_in, 1)
            pe.wait_ge(loaded, 16 * WEIGHT_DMAS)

            def turn(u, k):
                b = k % 2
                pe.wait_ge(basis_staged, u + 1)
                if k >= 1:
                    pe.wait_ge(hid1_ready, u)
                pe.transpose(ps_hid[0:G * NB, 2, :], basis[:, b, :], ident[:, :]).then_inc(basisT_ps, 1)
                if k >= 1:
                    pe.wait_ge(same_ready, u)
                for i in range(G):
                    mm = pe.transpose(ps_dst[:, i, :], dst_now[:, b, i:i + 1].broadcast_to([P, P]), ident[:, :])
                mm.then_inc(dst_ps, 1)
                pe.wait_ge(gathered[b], u * (16 * G // 2) + 16 * G - 16 * G * b // 2)
                if k >= 1:
                    pe.wait_ge(senderT_ready, u)
                for i in range(G):
                    mm = pe.transpose(ps_sT[:, P * i:P * (i + 1)], sender[:, k % RING, i, :], ident[:, :])
                mm.then_inc(senderT_ps, 1)

            def hidden0(u, k):
                b = k % 2
                pe.wait_ge(basisT_ready, u + 1)
                for q in range(2):
                    mm = pe.matmul(ps_hid[:, q, :], mlp0[:, q, :], basisT[:, b, :], start=True, stop=True)
                mm.then_inc(hid0_ps, 1)

            def hidden1(u, k):
                pe.wait_ge(hid0_ready, u + 1)
                pe.matmul(ps_hid[:, 2:4, :], mlp1[:, :], hid0[:, k % 2, :], start=True, stop=True
                          ).then_inc(hid1_ps, 1)

            def project_up(u, k):
                b = k % 2
                pe.wait_ge(senderT_ready, u + 1)
                if k >= 1:
                    pe.wait_ge(up_used, u)
                for i in range(G):
                    mm = pe.matmul(ps_up[:, i, :], senderT[:, b, P * i:P * (i + 1)], up[:, :], start=True, stop=True)
                mm.then_inc(up_ps, 1)

            def radial(u, k):
                b = k % 2
                pe.wait_ge(hid1_ready, u + 1)
                for i in range(G):
                    mm = pe.matmul(ps_wts[:, i, :], hid1[:, b, P * (i // 2):P * (i // 2 + 1)], mlp2[:, i % 2, :],
                                   start=True, stop=True)
                mm.then_inc(wts_ps, 1)

            def sums(v, k, r):
                b = k % 2
                if r == 0:
                    pe.wait_ge(mid_ready, v + 1)
                if k >= 1:
                    pe.wait_ge(sum_ready[r], v)
                for i in range(2):
                    for h in range(2):
                        mm = pe.matmul(ps_sum[r][:, i, h, :], mid[:, b, 2 * r + i, P * h:P * (h + 1)],
                                       same[:, b, 2 * r + i, :], start=True, stop=True)
                mm.then_inc(sum_ps[r], 1)

            def project_out(v, k):
                b = k % 2
                if k >= 1:
                    pe.wait_ge(msg_ready, v)
                for i in range(G):
                    if i % 2 == 0:
                        pe.wait_ge(sum_ready[i // 2], v + 1)
                    for h in range(2):
                        mm = pe.matmul(ps_msg[:, i, 2 * MUL * h:2 * MUL * (h + 1)], sumT[:, b, i, h, :],
                                       outw[:, h, :], start=True, stop=True)
                mm.then_inc(msg_ps, 1)

            def unit(u, k, following=True, tail=False):
                if not tail:
                    hidden0(u, k)
                    project_up(u, k)
                if k >= 1:
                    sums(u - 1, k - 1, 0)
                if not tail:
                    hidden1(u, k)
                if k >= 1:
                    sums(u - 1, k - 1, 1)
                if not tail:
                    radial(u, k)
                if following and not tail:
                    turn(u + 1, k + 1)
                if k >= 1:
                    project_out(u - 1, k - 1)

            turn(0, 0)
            for u in range(RING):
                unit(u, u)
            with pe.Fori(1, (UNITS - 2) // RING) as j:
                for k in range(RING):
                    unit(RING * j + k, RING + k)
            unit(UNITS - 2, UNITS - 2)
            unit(UNITS - 1, UNITS - 1, following=False)
            unit(UNITS, UNITS, tail=True)

        @block.scalar
        def _(act):
            load_edges(act, [(src_raw, src, 1), (len_raw, edge_len, 1)])
            for b in range(2):
                act.dma_start(start[:, b:b + 1], column(b0)).then_inc(stored[b], 16)
            len_units = len_all[:, :].rearrange("p (v i) -> p v i", i=G)
            vec_units = vec_all[:, :, :].rearrange("p (v i) c -> p v i c", i=G)
            for k, (a, to) in enumerate([(ps_len, len_units)] + [(ps_vec[c], vec_units[:, :, :, c]) for c in range(3)]):
                act.wait_ge(planes, 3 + k)
                for w in range(2):
                    mm = act.copy(turns(to, w), row_tiles(a, w))
                mm.then_inc(act_planes, 1)
            def prepare(n):
                t0, t1 = SPANS[n]
                act.wait_ge(dve_pre, PRE * n + 3)
                for k in range(NB):
                    mm = act.activation(basis_all[:, t0:t1, k], len_clip[:, t0:t1], ACT.Square, scale=float(NB - 1),
                                        bias=minus_k[:, k:k + 1])
                mm.then_inc(act_pre, 1)
                act.wait_ge(act_pre, 3 * n + 1)
                act.activation(basis_all[:, t0:t1, :], basis_all[:, t0:t1, :], ACT.Exp, scale=-0.5
                               ).then_inc(act_pre, 1)
                act.wait_ge(dve_pre, PRE * n + 5)
                act.activation(norm[:, t0:t1], norm[:, t0:t1], ACT.Sqrt).then_inc(act_pre, 1)

            prepare(0)
            act.wait_ge(loaded, 16 * WEIGHT_DMAS)
            act.mul(up[:, :], up_raw[:, :], MUL ** -0.5).then_inc(weights, 1)
            act.mul(mlp0[:, :, :], mlp0_raw[:, :, :], NB ** 0.5).then_inc(weights, 1)
            by = 1.0 / (AVG * (2 * MUL) ** 0.5)
            for k in range(4):
                for h in range(2):
                    rows = slice(MUL * k, MUL * (k + 1))
                    y = 3 ** 0.5 if k == 2 or (k == 0 and h == 1) else 1.0
                    mm = act.mul(outw[rows, h, :], out_raw[rows, h, :], by * y)
                mm.then_inc(weights, 1)

            def stage(u, k):
                b = k % 2
                act.copy(basis[:, b, :].rearrange("p (i k) -> p i k", k=NB), basis_all[:, bass.ds(u * G, G), :])
                act.copy(dst_now[:, b, :], dst_all[:, bass.ds(u, 1), :].rearrange("p v i -> p (v i)")
                         ).then_inc(basis_staged, 1)

            def sums_out(v, k, r):
                b = k % 2
                act.wait_ge(sum_ps[r], v + 1)
                act.copy(sumT[:, b, 2 * r:2 * r + 2, :, :], ps_sum[r][:, :, :, :]).then_inc(sum_ready[r], 1)

            def msg_out(v, k):
                b = k % 2
                act.wait_ge(msg_ps, v + 1)
                slot = bass.ds(v % RING, 1)
                if k >= RING:
                    for i in range(2, G):
                        act.wait_ge(scattered[b][i], 8 * (v - b) - 8 * RING + 16)
                act.copy(msg[:, slot, :, 0:MUL].rearrange("p s i k -> p (s i) k"), ps_msg[:, :, 0:MUL])
                act.copy(msg[:, slot, :, MUL:D].rearrange("p s i (k c) -> p (s i) c k", c=3),
                         ps_msg[:, :, MUL:D].rearrange("p i (c k) -> p i c k", c=3)).then_inc(msg_ready, 1)

            def turned(u, k, stage_next=True):
                b = k % 2
                act.wait_ge(basisT_ps, u + 1)
                act.copy(basisT[:, b, :], ps_hid[0:G * NB, 2, :]).then_inc(basisT_ready, 1)
                act.wait_ge(senderT_ps, u + 1)
                act.copy(senderT[:, b, :], ps_sT[:, :]).then_inc(senderT_ready, 1)
                if stage_next:
                    stage(u + 2, k)

            def unit(u, k, tail=False):
                b = k % 2
                if not tail:
                    act.wait_ge(hid0_ps, u + 1)
                    act.activation(hid0[:, b, :], ps_hid[:, 0:2, :].rearrange("p q e -> p (q e)"), ACT.Silu,
                                   bias=bias0[:, :]).then_inc(hid0_ready, 1)
                if k >= 1:
                    sums_out(u - 1, k - 1, 0)
                if not tail:
                    act.wait_ge(hid1_ps, u + 1)
                    act.activation(hid1[:, b, :], ps_hid[:, 2:4, :].rearrange("p q e -> p (q e)"), ACT.Silu,
                                   bias=bias1[:, :]).then_inc(hid1_ready, 1)
                if k >= 1:
                    sums_out(u - 1, k - 1, 1)
                if not tail and not (isinstance(u, int) and u + 1 >= UNITS):
                    turned(u + 1, k + 1, stage_next=not isinstance(u, int) or u + 3 < UNITS)
                if k >= 1:
                    msg_out(u - 1, k - 1)

            act.wait_ge(prepared, 4)
            act.wait_ge(act_pre, 2)
            act.sem_inc(stats_ready, 2)
            act.sem_inc(normed_ready, 4)

            def normalise(h, b, part, rows=ROWS, parts=P, store=False):
                c = 2 * h + b
                if part == 0:
                    act.wait_ge(shift_ready, c + 1)
                    act.wait_ge(stored[b], 16 * h + 16)
                quarter = bass.ds(2 * (h % 2) + b, 1)
                half = (rows + 1) // 2
                for r in (range(half, rows) if part else range(half)):
                    mm = act.activation(normed[0:parts, b, r, :],
                                        total[0:parts, quarter, r, :].rearrange("p b d -> p (b d)"), ACT.Identity,
                                        scale=rstd[0:parts, b, r:r + 1], bias=shift[0:parts, b, r:r + 1])
                if part == 0 and rows > 1:
                    return
                mm.then_inc(normed_ready, 1)
                if not store:
                    return
                act.wait_ge(normed_ready, c + 5)
                if parts == P:
                    to = out[bass.ds(N - CHUNK - c * CHUNK, CHUNK), :].rearrange("(p r) d -> p (r d)", p=P)
                    act.dma_start(to, normed[:, b, :, :].rearrange("p r d -> p (r d)")).then_inc(stored[b], 16)
                else:
                    act.dma_start(out[0:parts, :], normed[0:parts, b, 0, :]).then_inc(stored[b], 16)

            def pair(j, k):
                order = act.value_load(dense_orders[0:1, bass.ds(j, 1)], min_val=0, max_val=2 * CHUNKS - 2)
                for part in range(2):
                    unit(2 * j + part, k + part)
                    for b in range(2):
                        with act.If((order // 2 if b else order) % 2):
                            normalise(order // 4, b, part)

            stage(0, 0)
            stage(1, 1)
            turned(0, 0)
            unit(0, 0)
            prepare(1)
            act.wait_ge(act_pre, 5)
            first = RING // 2 + 1
            for u in range(1, 2 * first):
                unit(u, u)
            act.wait_ge(tables, 1)
            with act.Fori(first, PAIRS - 2) as j:
                pair(j, 2 * first)
            for j in range(PAIRS - 2, PAIRS):
                pair(j, 2 * j)
            unit(UNITS, UNITS, tail=True)
            done = act.value_load(done_count[0:1, 2:3], min_val=0, max_val=CHUNKS - 1)
            with act.If(done % 2):
                for part in range(2):
                    normalise(done // 2, 1, part, store=True)
            with act.If(CHUNKS - 1 - done):
                with act.Fori((done + 1) // 2, CHUNKS // 2) as h:
                    for b in range(2):
                        for part in range(2):
                            normalise(h, b, part, store=True)
            normalise(CHUNKS // 2, 0, 0, 1, REST, store=True)

        @block.vector
        def _(dve):
            dve.memset(zeros[:, :, :], 0.0).then_inc(zeroed, 1)
            dve.wait_ge(edges_in, 16 * 12)
            dve.tensor_copy(src_rawf[:, :, :], src_raw[:, :, :])
            dve.tensor_copy(dst_rawf[:, :, :], dst_raw[:, :, :]).then_inc(edges_f32, 1)
            dve.wait_ge(edges_f32, 1)
            dve.tensor_reduce(low_raw[:, :], dst_rawf[:, :, :], AX_X, ALU.min).then_inc(tile_ends, 1)
            dve.tensor_reduce(high_raw[:, :], dst_rawf[:, :, :], AX_X, ALU.max).then_inc(tile_ends, 1)
            dve.wait_ge(planes, 1)
            for w in range(2):
                mm = dve.tensor_copy(turns(index[:, 0:UNITS, 0, :], w), row_tiles(ps_src, w))
            mm.then_inc(index_in, 1)
            dve.wait_ge(planes, 2)
            for w in range(2):
                dve.tensor_copy(turns(dst_all[:, :, :], w), row_tiles(ps_dst, w)).then_inc(prepared, 1)
            dve.wait_ge(ends_ps, 2)
            for w in range(2):
                dve.tensor_scalar(turns(low[:, :, :], w), row_tiles(ps_high[0:1, :, :], w), -1.0, float(N - 1),
                                  ALU.mult, ALU.add)
                mm = dve.tensor_scalar(turns(high[:, :, :], w), row_tiles(ps_low[0:1, :, :], w), -1.0, float(N - 1),
                                       ALU.mult, ALU.add)
            mm.then_inc(prepared, 1)
            dve.wait_ge(act_planes, 4)
            dve.tensor_copy(dump_rowf[:, :], dump_row[:, :]).then_inc(dump_ready, 1)
            dve.wait_ge(prepared, 2)
            dve.wait_ge(dump_ready, 1)
            dve.tensor_tensor(gap_all[:, :, :].rearrange("p v (h r) -> p (v h) r", r=2),
                              wide(dump_rowf[:, :], 1, TILES // 2),
                              dst_all[:, :, :].rearrange("p v (h r) -> p (v h) r", r=2), ALU.subtract
                              ).then_inc(prepared, 1)

            def prepare(n):
                t0, t1 = SPANS[n]
                tiles, first = slice(t0, t1), PRE * n
                dve.tensor_scalar(len_clip[:, tiles], len_all[:, tiles], 0.0, 1.0, ALU.max, ALU.min
                                  ).then_inc(dve_pre, 1)
                dve.tensor_scalar(beyond[:, tiles], len_all[:, tiles], 1.0, FAR, ALU.is_gt, ALU.mult
                                  ).then_inc(dve_pre, 1)
                dve.wait_ge(dve_pre, first + 2)
                dve.tensor_tensor(len_clip[:, tiles], len_clip[:, tiles], beyond[:, tiles], ALU.add
                                  ).then_inc(dve_pre, 1)
                dve.tensor_tensor(vec_sq[:, tiles, :], vec_all[:, tiles, :], vec_all[:, tiles, :], ALU.mult
                                  ).then_inc(dve_pre, 1)
                dve.wait_ge(dve_pre, first + 4)
                dve.tensor_reduce(norm[:, tiles], vec_sq[:, tiles, :], AX_X, ALU.add).then_inc(dve_pre, 1)

            def directions(n):
                t0, t1 = SPANS[n]
                tiles, first = slice(t0, t1), PRE * n
                dve.wait_ge(act_pre, 3 * n + 3)
                dve.tensor_scalar(norm[:, tiles], norm[:, tiles], 1e-12, None, ALU.add).then_inc(dve_pre, 1)
                dve.wait_ge(dve_pre, first + 6)
                dve.reciprocal(norm[:, tiles], norm[:, tiles]).then_inc(dve_pre, 1)
                dve.wait_ge(dve_pre, first + 7)
                dve.tensor_tensor(vec_all[:, tiles, :], vec_all[:, tiles, :], wide(norm[:, tiles], 2, 3), ALU.mult
                                  ).then_inc(directions_ready, 1)
                dve.wait_ge(directions_ready, n + 1)

            dve.wait_ge(act_planes, 4)
            prepare(0)
            directions(0)
            dve.wait_ge(loaded, 16 * WEIGHT_DMAS)

            def equal_receivers(u, k):
                b = k % 2
                dst_col = dst_all[:, bass.ds(u, 1), :].rearrange("p v i -> p (v i)")
                dve.wait_ge(dst_ps, u + 1)
                if k >= 2:
                    dve.wait_ge(sum_ps[1], u - 1)
                dve.tensor_tensor(same[:, b, :, :], ps_dst[:, :, :], wide(dst_col, 2, P), ALU.is_equal
                                  ).then_inc(same_ready, 1)
                dve.wait_ge(same_ready, u + 1)
                for i in range(G):
                    mm = dve.tensor_tensor_reduce(junk[:, b, i, :], same[:, b, i, :], earlier[:, :], 1.0, 0.0,
                                                  ALU.mult, ALU.add, count[:, b, i:i + 1])
                mm.then_inc(counted, 1)

            def receiver_rows(u, k, step):
                b = k % 2
                if step == 0:
                    dve.wait_ge(counted, u + 1)
                    dve.scalar_tensor_tensor(out=rowf[:, b, :], in0=count[:, b, :], scalar=1.0,
                                             in1=gap_all[:, bass.ds(u, 1), :].rearrange("p v i -> p (v i)"),
                                             op0=ALU.min, op1=ALU.mult).then_inc(rowf_ready, 1)
                else:
                    dve.wait_ge(rowf_ready, u + 1)
                    dve.tensor_tensor(index[:, bass.ds(u + LAG, 1), 1, :].rearrange("p s i -> p (s i)"),
                                      rowf[:, b, :], dst_all[:, bass.ds(u, 1), :].rearrange("p v i -> p (v i)"),
                                      ALU.add).then_inc(rows_ready, 1)

            def products(u, k):
                b = k % 2
                y = vec_all[:, bass.ds(u * G, G), :]
                w, md = wts[:, b, :, :], mid[:, b, :, :]
                s, v = ps_up[:, :, 0:MUL], ps_up[:, :, MUL:D].rearrange("p i (c k) -> p i c k", c=3)
                pairs = md[:, :, 0:8 * MUL].rearrange("p i (c k) -> p i c k", c=4)
                pj = proj[:, b, :, :].rearrange("p i (c k) -> p i c k", c=3)
                dve.wait_ge(wts_ps, u + 1)
                dve.tensor_tensor(w, ps_wts[:, :, :], wide(bias2[:, :], 1, G), ALU.add).then_inc(wts_ready, 1)
                dve.wait_ge(up_ps, u + 1)
                dve.tensor_tensor(pj, v, wide(y, 3, MUL), ALU.mult).then_inc(dve_step, 1)
                receiver_rows(u, k, 0)
                dve.wait_ge(wts_ready, u + 1)
                dve.tensor_tensor(md[:, :, 0:MUL], w[:, :, 0:MUL], s, ALU.mult)
                dve.tensor_tensor(md[:, :, 8 * MUL:9 * MUL], w[:, :, MUL:2 * MUL], s, ALU.mult
                                  ).then_inc(dve_step, 1)
                dve.tensor_tensor(pairs[:, :, 1:4, MUL:2 * MUL], v, wide(w[:, :, 2 * MUL:3 * MUL], 2, 3), ALU.mult
                                  ).then_inc(up_used, 1)
                dve.wait_ge(dve_step, 2 * u + 2)
                dve.tensor_reduce(dot[:, b, :, :], pj.rearrange("p i c k -> p i k c"), AX_X, ALU.add
                                  ).then_inc(dve_step_dot, 1)
                receiver_rows(u, k, 1)
                dve.tensor_tensor(pairs[:, :, 1:4, 0:MUL], wide(md[:, :, 8 * MUL:9 * MUL], 2, 3), wide(y, 3, MUL),
                                  ALU.mult)
                dve.wait_ge(dve_step_dot, u + 1)
                dve.tensor_tensor(md[:, :, MUL:2 * MUL], w[:, :, 3 * MUL:D], dot[:, b, :, :], ALU.mult
                                  ).then_inc(mid_ready, 1)

            def unit(u, k, following=True):
                products(u, k)
                if following:
                    equal_receivers(u + 1, k + 1)

            def make_orders():
                steps = [0]

                def link(ins):
                    steps[0] += 1
                    ins.then_inc(table_step, 1)
                    dve.wait_ge(table_step, steps[0])

                lo, hi = (a[:, :, :].rearrange("p v i -> p (v i)") for a in (low, high))
                by_unit = meet[:, :].rearrange("p (v i) -> p v i", i=G)
                link(dve.tensor_tensor(meet[:, 1:TILES], hi[:, 0:TILES - 1], lo[:, 1:TILES], ALU.is_ge))
                link(dve.tensor_tensor(meet_too[:, 1:TILES], hi[:, 1:TILES], lo[:, 0:TILES - 1], ALU.is_ge))
                link(dve.tensor_tensor(meet[:, 1:TILES], meet[:, 1:TILES], meet_too[:, 1:TILES], ALU.mult))
                link(dve.tensor_reduce(meet_unit[:, :], by_unit[:, :, 1:G], AX_X, ALU.max))
                link(dve.tensor_reduce(pieces[:, :], high[:, :, :], AX_X, ALU.max))
                link(dve.tensor_scalar(piece_int[:, :], pieces[:, :], -(PIECE - 1) / 2, 1.0 / PIECE, ALU.add, ALU.mult))
                link(dve.tensor_copy(pieces[:, :], piece_int[:, :]))
                link(dve.tensor_scalar(pieces[:, :], pieces[:, :], 1.0, float(PIECES - 1), ALU.max, ALU.min))
                link(dve.tensor_scalar(pieces[:, :], pieces[:, :], 4.0, None, ALU.mult))
                link(dve.scalar_tensor_tensor(out=orders[:, :], in0=meet_unit[:, :], scalar=2.0, in1=pieces[:, :],
                                              op0=ALU.mult, op1=ALU.add))
                link(dve.tensor_tensor(scatter_orders[:, :], orders[:, :], by_unit[:, :, 0], ALU.add))
                link(dve.tensor_reduce(least[0][:, 0:UNITS], low[:, :, :], AX_X, ALU.min))
                link(dve.tensor_copy(least[1][:, 0:UNITS], least[0][:, 1:UNITS + 1]))
                now, reach = 1, 1
                link(dve.tensor_scalar(least[0][:, 0:UNITS], least[1][:, 0:UNITS], float(N), None, ALU.min))
                now = 0
                while reach < UNITS:
                    link(dve.tensor_tensor(least[1 - now][:, 0:UNITS], least[now][:, 0:UNITS],
                                           least[now][:, reach:UNITS + reach], ALU.min))
                    now, reach = 1 - now, 2 * reach
                by_pair = least[now][:, 0:UNITS].rearrange("p (j b) -> p j b", b=2)[:, :, 1]
                link(dve.tensor_scalar(final_int[:, :], by_pair, -(CHUNK - 1) / 2, 1.0 / CHUNK, ALU.add, ALU.mult))
                link(dve.tensor_copy(rising[:, :], final_int[:, :]))
                link(dve.tensor_scalar(rising[:, :], rising[:, :], float(CHUNKS - 1), None, ALU.min))
                link(dve.memset(rising[:, 0:DENSE_FROM], 0.0))
                link(dve.scalar_tensor_tensor(out=least[0][:, P:P + PAIRS], in0=by_index[:, :], scalar=-RATE,
                                              in1=rising[:, :], op0=ALU.mult, op1=ALU.add))
                now, reach = 0, 1
                while reach < PAIRS:
                    link(dve.tensor_tensor(least[1 - now][:, P:P + PAIRS], least[now][:, P:P + PAIRS],
                                           least[now][:, P - reach:P + PAIRS - reach], ALU.min))
                    now, reach = 1 - now, 2 * reach
                link(dve.scalar_tensor_tensor(out=least[now][:, P:P + PAIRS], in0=by_index[:, :], scalar=RATE,
                                              in1=least[now][:, P:P + PAIRS], op0=ALU.mult, op1=ALU.add))
                link(dve.tensor_scalar(final_int[:, :], least[now][:, P:P + PAIRS], -0.4, None, ALU.add))
                link(dve.tensor_copy(final[:, 1:1 + PAIRS], final_int[:, :]))
                for k, after in enumerate((0, STATS_AFTER, NORM_AFTER)):
                    dve.tensor_copy(done_count[:, k:k + 1], final[:, PAIRS - after:PAIRS - after + 1])
                link(dve.tensor_tensor(fresh[:, :], final[:, 1:1 + PAIRS], final[:, 0:PAIRS], ALU.subtract))
                link(dve.tensor_scalar(rising[:, :], final[:, 1:1 + PAIRS], -1.0, 0.0, ALU.add, ALU.max))
                link(dve.tensor_scalar(final_int[:, :], rising[:, :], -0.5, 0.5, ALU.add, ALU.mult))
                link(dve.tensor_copy(half_chunk[:, :], final_int[:, :]))
                link(dve.scalar_tensor_tensor(out=rising[:, :], in0=half_chunk[:, :], scalar=-2.0, in1=rising[:, :],
                                              op0=ALU.mult, op1=ALU.add))
                link(dve.scalar_tensor_tensor(out=fresh[:, :], in0=rising[:, :], scalar=1.0, in1=fresh[:, :],
                                              op0=ALU.add, op1=ALU.mult))
                dve.scalar_tensor_tensor(out=dense_orders[:, NORM_AFTER:NORM_AFTER + PAIRS], in0=half_chunk[:, :],
                                         scalar=4.0, in1=fresh[:, :], op0=ALU.mult, op1=ALU.add).then_inc(tables, 1)
                dve.wait_ge(tables, 1)

            def moments(h, b, rows=ROWS, parts=P):
                c = 2 * h + b
                quarter = bass.ds(2 * (h % 2) + b, 1)
                dve.wait_ge(total_in[b], 16 * h + 16)
                for r in range(rows):
                    mm = dve.bn_stats(stats[0:parts, r, :], total[0:parts, quarter, r, :].rearrange("p b d -> p (b d)"))
                mm.then_inc(stats_ready, 1)

            def statistics(h, b, rows=ROWS, parts=P):
                c = 2 * h + b
                st = stats[0:parts, 0:rows, :]
                mn, hg, gs = (a[0:parts, 0:rows] for a in (mean, half_gap, gap_sq))
                vr, rs, sh, bt = (a for a in (var[0:parts, 0:rows], rstd[0:parts, b, 0:rows],
                                              shift[0:parts, b, 0:rows], bits[0:parts, 0:rows]))
                step = SSTEPS * c
                dve.wait_ge(stats_ready, c + 3)
                dve.tensor_tensor(mn, st[:, :, 1], st[:, :, 4], ALU.add)
                dve.tensor_tensor(vr, st[:, :, 2], st[:, :, 5], ALU.add)
                dve.tensor_tensor(hg, st[:, :, 1], st[:, :, 4], ALU.subtract).then_inc(stat_step, 1)
                dve.wait_ge(stat_step, step + 1)
                dve.scalar_tensor_tensor(out=gs, in0=hg, scalar=0.25, in1=hg, op0=ALU.mult, op1=ALU.mult)
                dve.tensor_scalar(vr, vr, 1.0 / D, EPS, ALU.mult, ALU.add).then_inc(stat_step, 1)
                dve.wait_ge(stat_step, step + 2)
                dve.tensor_tensor(vr, vr, gs, ALU.add).then_inc(stat_step, 1)
                dve.wait_ge(stat_step, step + 3)
                dve.tensor_scalar(bt, vr.bitcast(I32), 1, None, ALU.logical_shift_right).then_inc(stat_step, 1)
                dve.wait_ge(stat_step, step + 4)
                dve.wait_ge(normed_ready, c + 3)
                dve.tensor_scalar(rs.bitcast(I32), bt, -1.0, RSQRT_BITS, ALU.mult, ALU.add).then_inc(stat_step, 1)
                for k in range(ROUNDS):
                    dve.wait_ge(stat_step, step + 5 + 3 * k)
                    dve.tensor_tensor(gs, rs, rs, ALU.mult).then_inc(stat_step, 1)
                    dve.wait_ge(stat_step, step + 6 + 3 * k)
                    dve.scalar_tensor_tensor(out=gs, in0=gs, scalar=-0.5, in1=vr, op0=ALU.mult, op1=ALU.mult
                                             ).then_inc(stat_step, 1)
                    dve.wait_ge(stat_step, step + 7 + 3 * k)
                    dve.scalar_tensor_tensor(out=rs, in0=gs, scalar=1.5, in1=rs, op0=ALU.add, op1=ALU.mult
                                             ).then_inc(stat_step, 1)
                dve.wait_ge(stat_step, step + SSTEPS)
                dve.scalar_tensor_tensor(out=sh, in0=mn, scalar=-0.5, in1=rs, op0=ALU.mult, op1=ALU.mult
                                         ).then_inc(shift_ready, 1)

            def pair(j, k, last=False):
                order = dve.value_load(dense_orders[0:1, bass.ds(j + NORM_AFTER - STATS_AFTER, 1)], min_val=0,
                                       max_val=2 * CHUNKS - 2)
                for part in range(2):
                    unit(2 * j + part, k + part, following=part == 0 or not last)
                    for b in range(2):
                        with dve.If((order // 2 if b else order) % 2):
                            (statistics if part else moments)(order // 4, b)

            equal_receivers(0, 0)
            unit(0, 0)
            prepare(1)
            make_orders()
            unit(1, 1)
            unit(2, 2)
            directions(1)
            unit(3, 3)
            with dve.Fori(2, PAIRS - 1) as j:
                pair(j, 4)
            pair(PAIRS - 1, UNITS - 2, last=True)
            done = dve.value_load(done_count[0:1, 1:2], min_val=0, max_val=CHUNKS - 1)
            with dve.If(done % 2):
                moments(done // 2, 1)
                statistics(done // 2, 1)
            with dve.If(CHUNKS - 1 - done):
                with dve.Fori((done + 1) // 2, CHUNKS // 2) as h:
                    for b in range(2):
                        moments(h, b)
                        statistics(h, b)
            moments(CHUNKS // 2, 0, 1, REST)
            statistics(CHUNKS // 2, 0, 1, REST)


_INS = ['x', 'src', 'dst', 'edge_attr_3', 'edge_weight', 'L0_gnn_W_up0', 'L0_gnn_W_up1', 'L0_gnn_mlp_w0',
        'L0_gnn_mlp_b0', 'L0_gnn_mlp_w1', 'L0_gnn_mlp_b1', 'L0_gnn_mlp_w2', 'L0_gnn_mlp_b2', 'L0_gnn_W_out0',
        'L0_gnn_W_out1']


def kernel(**inputs):
    import numpy as _np
    import concourse.bacc as _bacc
    from concourse import mybir as _mybir
    from concourse.bass_utils import run_bass_kernel_spmd as _run

    nc = _bacc.Bacc("TRN2", target_bir_lowering=False, num_devices=1)
    arrays, args = {}, []
    for name in _INS:
        a = _np.ascontiguousarray(inputs[name])
        arrays[f"in_{name}_dram"] = a
        args.append(nc.dram_tensor(f"in_{name}_dram", a.shape, _mybir.dt.from_np(a.dtype), kind="ExternalInput").ap())
    args.append(nc.dram_tensor("out_0_dram", (N, D), F32, kind="ExternalOutput").ap())
    bass_gnn(nc, *args)
    r = _run(nc, [arrays], core_ids=[0])
    return r.results[0]["out_0_dram"]
```

```python
from contextlib import ExitStack

import concourse.bass as bass
from concourse import mybir
from concourse.alu_op_type import AluOpType as ALU

F32 = mybir.dt.float32
I32 = mybir.dt.int32
ACT = mybir.ActivationFunctionType
AX_X = mybir.AxisListType.X

P = 128
N = 50000
E = 50000
D = 128
MUL = 32
NB = 8
HID = 64
AVG = 16.0
EPS = 1e-5

G = 4
ROWE = G * P
UNITS = -(-E // ROWE)
FULL = E // ROWE
TILES = UNITS * G
PAIRS = UNITS // 2
LAG = 6
RING = 4
STATS_AFTER = 4
NORM_AFTER = STATS_AFTER + 1
RATE = 3 / 4
DENSE_FROM = 4
FAR = 100.0
SPARE = 3 * P
MIDW = 9 * MUL

ROWS = 13
CHUNK = P * ROWS
CHUNKS = N // CHUNK
REST = N - CHUNKS * CHUNK
PIECE = 625
PIECES = N // PIECE
PIECES_FIRST = 2
ROUNDS = 3
SSTEPS = 5 + 3 * ROUNDS
RSQRT_BITS = float(0x5f3759df)
assert UNITS % 2 == 0 and LAG % 2 == 0 and UNITS <= P and FULL == UNITS - 1 and FULL >= 96
assert NORM_AFTER > STATS_AFTER and NORM_AFTER > RING // 2 and RING % 2 == 0 and (UNITS - 2) % RING == 0
assert CHUNKS % 2 == 0 and PIECES % 2 == 0 and N % PIECE == 0 and REST <= P


def bass_gnn(nc, x, src, dst, edge_vec, edge_len, W_up0, W_up1, w0, b0, w1, b1, w2, b2, W_out0, W_out1, out):
    acc = nc.dram_tensor("acc", (N + SPARE, D), F32, kind="Internal").ap()

    ctx = ExitStack()
    with ctx:
        def sb(name, shape, dt=F32):
            return ctx.enter_context(nc.sbuf_tensor(name, shape, dt))

        def psum(name, shape):
            return ctx.enter_context(nc.psum_tensor(name, shape, F32))

        def sem(name):
            return ctx.enter_context(nc.semaphore(name))

        ident = sb("ident", [P, P])
        backward = sb("backward", [P, P])
        earlier = sb("earlier", [P, P])
        dump_row = sb("dump_row", [P, 2], I32)
        dump_rowf = sb("dump_rowf", [P, 2])
        zeros = sb("zeros", [P, SPARE // P, D])
        minus_k = sb("minus_k", [P, NB])
        up_raw = sb("up_raw", [P, D])
        up = sb("up", [P, D])
        mlp0_raw = sb("mlp0_raw", [G * NB, 2, 2 * HID])
        mlp0 = sb("mlp0", [G * NB, 2, 2 * HID])
        mlp1 = sb("mlp1", [2 * HID, 2 * HID])
        mlp2 = sb("mlp2", [2 * HID, 2, D])
        start = sb("start", [HID, 2])
        bias0 = sb("bias0", [2 * HID, 1])
        bias1 = sb("bias1", [2 * HID, 1])
        bias2 = sb("bias2", [P, D])
        out_raw = sb("out_raw", [P, 2, 2 * MUL])
        outw = sb("outw", [P, 2, 2 * MUL])
        src_raw = sb("src_raw", [UNITS, G, P], I32)
        dst_raw = sb("dst_raw", [UNITS, G, P], I32)
        src_rawf = sb("src_rawf", [UNITS, G, P])
        dst_rawf = sb("dst_rawf", [UNITS, G, P])
        len_raw = sb("len_raw", [UNITS, G, P])
        vec_raw = sb("vec_raw", [UNITS, G, P, 3])
        low_raw = sb("low_raw", [UNITS, G])
        high_raw = sb("high_raw", [UNITS, G])
        low = sb("low", [1, UNITS, G])
        high = sb("high", [1, UNITS, G])
        meet = sb("meet", [1, TILES])
        meet_too = sb("meet_too", [1, TILES])
        floor_int = sb("floor_int", [1, UNITS], I32)
        too_much = sb("too_much", [1, UNITS])
        deepest = sb("deepest", [1, UNITS])
        pieces = sb("pieces", [1, UNITS])
        meet_unit = sb("meet_unit", [1, UNITS])
        by_index = sb("by_index", [1, PAIRS])
        orders = sb("orders", [1, UNITS])
        scatter_orders = sb("scatter_orders", [1, UNITS], I32)
        AT = UNITS + P - PAIRS
        least = [sb(f"least{k}", [1, 2 * P]) for k in range(2)]
        rising = sb("rising", [1, PAIRS])
        final = sb("final", [1, 1 + PAIRS])
        fresh = sb("fresh", [1, PAIRS])
        half_chunk = sb("half_chunk", [1, PAIRS])
        dense_orders = sb("dense_orders", [1, NORM_AFTER + PAIRS], I32)
        done_count = sb("done_count", [1, 3], I32)
        dst_all = sb("dst_all", [P, UNITS, G])
        gap_all = sb("gap_all", [P, UNITS, G])
        index = sb("index", [P, UNITS + LAG, 2, G], I32)
        vec_all = sb("vec_all", [P, TILES, 3])
        vec_sq = sb("vec_sq", [P, TILES, 3])
        norm = sb("norm", [P, TILES])
        len_all = sb("len_all", [P, TILES])
        beyond = sb("beyond", [P, TILES])
        len_clip = sb("len_clip", [P, TILES])
        basis_all = sb("basis_all", [P, TILES, NB])
        index_now = sb("index_now", [P, 2, 2, G], I32)
        sender = sb("sender", [P, RING, G, D])
        basis = sb("basis", [P, 2, G * NB])
        dst_now = sb("dst_now", [P, 2, G])
        basisT = sb("basisT", [G * NB, 2, P])
        senderT = sb("senderT", [P, 2, G * P])
        hid0 = sb("hid0", [2 * HID, 2, 2 * P])
        hid1 = sb("hid1", [2 * HID, 2, 2 * P])
        same = sb("same", [P, 2, G, P])
        junk = sb("junk", [P, 2, G, P])
        count = sb("count", [P, 2, G])
        rowf = sb("rowf", [P, 2, G])
        wts = sb("wts", [P, 2, G, D])
        mid = sb("mid", [P, 2, G, MIDW])
        proj = sb("proj", [P, 2, G, 3 * MUL])
        dot = sb("dot", [P, 2, G, MUL])
        sumT = sb("sumT", [P, 2, G, 2, P])
        msg = sb("msg", [P, RING, G, D])
        total = sb("total", [P, 4, ROWS, D])
        normed = sb("normed", [P, 2, ROWS, D])
        stats = sb("stats", [P, ROWS, 6])
        mean = sb("mean", [P, ROWS])
        half_gap = sb("half_gap", [P, ROWS])
        gap_sq = sb("gap_sq", [P, ROWS])
        var = sb("var", [P, ROWS])
        bits = sb("bits", [P, ROWS], I32)
        rstd = sb("rstd", [P, 2, ROWS])
        shift = sb("shift", [P, 2, ROWS])

        ps_hid = psum("ps_hid", [P, 4, P])
        ps_sT = psum("ps_sT", [P, G * P])
        ps_up = psum("ps_up", [P, G, D])
        ps_wts = psum("ps_wts", [P, G, D])
        ps_dst = psum("ps_dst", [P, G, P])
        ps_sum = [psum(f"ps_sum{r}", [P, 2, 2, P]) for r in range(2)]
        ps_msg = psum("ps_msg", [P, G, D])

        ps_src, ps_len, ps_low, ps_high = ps_sT[:, :].rearrange("p (i e) -> p i e", i=G), ps_wts, ps_msg, ps_hid
        ps_vec = [ps_up] + [a[:, :, :, :].rearrange("p i h e -> p (i h) e") for a in ps_sum]

        cleared = sem("cleared")
        consts = sem("consts")
        loaded = sem("loaded")
        edges_in = sem("edges_in")
        edges_f32 = sem("edges_f32")
        tile_ends = sem("tile_ends")
        planes = sem("planes")
        ends_ps = sem("ends_ps")
        act_planes = sem("act_planes")
        acc_init = [sem(f"acc_init{b}") for b in range(2)]
        spare_rows = sem("spare_rows")
        table_step = sem("table_step")
        scatter_tables = sem("scatter_tables")
        tables = sem("tables")
        dve_pre = sem("dve_pre")
        act_pre = sem("act_pre")
        dump_ready = sem("dump_ready")
        prepared = sem("prepared")
        directions_ready = sem("directions_ready")
        weights = sem("weights")
        zeroed = sem("zeroed")
        index_in = sem("index_in")
        pool_staged = sem("pool_staged")
        pool_passed = sem("pool_passed")
        sp_passed = sem("sp_passed")
        gathered = [sem(f"gathered{b}") for b in range(2)]
        basis_staged = sem("basis_staged")
        basisT_ps = sem("basisT_ps")
        senderT_ps = sem("senderT_ps")
        dst_ps = sem("dst_ps")
        basisT_ready = sem("basisT_ready")
        senderT_ready = sem("senderT_ready")
        hid0_ps = sem("hid0_ps")
        hid0_ready = sem("hid0_ready")
        hid1_ps = sem("hid1_ps")
        hid1_ready = sem("hid1_ready")
        up_ps = sem("up_ps")
        wts_ps = sem("wts_ps")
        up_used = sem("up_used")
        same_ready = sem("same_ready")
        rows_ready = sem("rows_ready")
        counted = sem("counted")
        rowf_ready = sem("rowf_ready")
        dve_step = sem("dve_step")
        dve_step_dot = sem("dve_step_dot")
        wts_ready = sem("wts_ready")
        mid_ready = sem("mid_ready")
        sum_ps = [sem(f"sum_ps{r}") for r in range(2)]
        sum_ready = [sem(f"sum_ready{r}") for r in range(2)]
        msg_ps = sem("msg_ps")
        msg_ready = sem("msg_ready")
        scattered = [[sem(f"scattered{b}_{i}") for i in range(G)] for b in range(2)]
        total_in = [sem(f"total_in{b}") for b in range(2)]
        stat_step = sem("stat_step")
        shift_ready = sem("shift_ready")
        stats_ready = sem("stats_ready")
        normed_ready = sem("normed_ready")
        stored = [sem(f"stored{b}") for b in range(2)]

        block = ctx.enter_context(nc.Block())
        WEIGHT_DMAS = 1 + 3 + G + 2 + 2 + 4 + 1 + 4

        def load_edges(engine, arrays):
            def load(to, v, w, r0, r1):
                flat = v if w == 1 else v.rearrange("e c -> (e c)")
                rows = to.rearrange("r q p -> r (q p)") if w == 1 else to.rearrange("r q p c -> r (q p c)")
                n = (min(E, r1 * ROWE) - r0 * ROWE) * w
                engine.dma_start(rows[r0:r1, 0:n // (r1 - r0)],
                                 flat[r0 * ROWE * w:r0 * ROWE * w + n].rearrange("(r e) -> r e", r=r1 - r0)
                                 ).then_inc(edges_in, 16)

            for a in arrays:
                load(*a, 0, 96)
            engine.wait_ge(cleared, 4)
            for a in arrays:
                load(*a, 96, FULL)
                load(*a, FULL, UNITS)

        def column(v):
            return v.rearrange("(k a) -> k a", a=1)

        def wide(a, axis, n):
            a = a.unsqueeze(axis)
            shape = list(a.shape)
            shape[axis] = n
            return a.broadcast_to(shape)

        def turns(a, w):
            return a.rearrange("p (j w) (q r) -> p w q j r", w=2, r=2)[:, w]

        def row_tiles(a, w):
            return a[:, 2 * w:2 * w + 2, 0:UNITS].rearrange("p q (j r) -> p q j r", r=2)

        @block.sync
        def _(sp):
            load_edges(sp, [(dst_raw[:, :, :], dst, 1), (vec_raw[:, :, :, :], edge_vec, 3)])
            sp.wait_ge(zeroed, 1)
            sp.dma_start(acc[N:N + SPARE, :].rearrange("(p k) d -> p k d", p=P), zeros[:, :, :]
                         ).then_inc(spare_rows, 16)

            def copy(h, b, waits=True):
                if waits:
                    sp.wait_ge(acc_init[b], 16 * h)
                    sp.sem_inc(sp_passed, 1)
                rows = bass.ds(N - PIECE - (2 * h + b) * PIECE, PIECE)
                to, of = (a[rows, :].rearrange("n d -> (n d)").rearrange("(p f) -> p f", p=P) for a in (acc, x))
                sp.dma_start(to, of).then_inc(acc_init[b], 16)

            for k in range(PIECES_FIRST):
                copy(k // 2, k % 2, waits=k >= 2)
            sp.wait_ge(consts, 1)
            sp.dma_start(up_raw[0:MUL, 0:MUL], W_up0).then_inc(loaded, 16)
            for c in range(3):
                rows = up_raw[MUL + c:MUL + c + 3 * (MUL - 1) + 1:3, MUL * (c + 1):MUL * (c + 2)]
                sp.dma_start(rows, W_up1).then_inc(loaded, 16)
            for i in range(G):
                sp.dma_start(mlp0_raw[NB * i:NB * (i + 1), i // 2, HID * (i % 2):HID * (i % 2 + 1)], w0
                             ).then_inc(loaded, 16)
            for s in range(2):
                half = slice(HID * s, HID * (s + 1))
                sp.dma_start(mlp1[half, half], w1).then_inc(loaded, 16)
                sp.dma_start(mlp2[half, s, :], w2).then_inc(loaded, 16)
                sp.dma_start(bias0[half, :], column(b0)).then_inc(loaded, 16)
                sp.dma_start(bias1[half, :], column(b1)).then_inc(loaded, 16)
            sp.dma_start(bias2[:, :], b2.partition_broadcast(P)).then_inc(loaded, 16)
            for h in range(2):
                for k in range(2):
                    w = W_out0 if h == 0 and k == 0 else W_out1
                    sp.dma_start(out_raw[2 * MUL * k:2 * MUL * (k + 1), h, MUL * k:MUL * (k + 1)], w
                                 ).then_inc(loaded, 16)
            with sp.Fori(PIECES_FIRST // 2, PIECES // 2) as h:
                for b in range(2):
                    copy(h, b)
            for b in range(2):
                sp.wait_ge(acc_init[b], 16 * (PIECES // 2))
            sp.wait_ge(tables, 1)

            def load(h, b):
                c = 2 * h + b
                sp.wait_ge(stats_ready, c + 1)
                sp.wait_ge(normed_ready, c + 1)
                sp.dma_start(total[:, bass.ds(2 * (h % 2) + b, 1), :, :].rearrange("p b r d -> p (b r d)"),
                             acc[bass.ds(N - CHUNK - c * CHUNK, CHUNK), :].rearrange("(p r) d -> p (r d)", p=P)
                             ).then_inc(total_in[b], 16)

            def landed(j):
                for b in range(2):
                    for i in range(2, G):
                        sp.wait_ge(scattered[b][i], 16 * j + 16)

            def store(h, b):
                c = 2 * h + b
                sp.wait_ge(normed_ready, c + 5)
                sp.sem_inc(sp_passed, 1)
                sp.dma_start(out[bass.ds(N - CHUNK - c * CHUNK, CHUNK), :].rearrange("(p r) d -> p (r d)", p=P),
                             normed[:, b, :, :].rearrange("p r d -> p (r d)")).then_inc(stored[b], 16)

            def orders_of(at):
                order = sp.value_load(dense_orders[0:1, bass.ds(at, 1)], min_val=0, max_val=2 * CHUNKS - 2)
                return [(order // 4, b, (order // 2 if b else order) % 2) for b in range(2)]

            def pair(j, stores=True):
                if stores:
                    for h, b, now in orders_of(j + 1):
                        with sp.If(now):
                            store(h, b)
                for h, b, now in orders_of(j + NORM_AFTER):
                    with sp.If(now):
                        landed(j)
                        load(h, b)

            with sp.Fori(0, PAIRS - 1) as j:
                pair(j)
            pair(PAIRS - 1, stores=False)
            landed(PAIRS - 1)
            done = sp.value_load(done_count[0:1, 0:1], min_val=0, max_val=CHUNKS - 1)
            with sp.If(done % 2):
                load(done // 2, 1)
            with sp.If(CHUNKS - 1 - done):
                with sp.Fori((done + 1) // 2, CHUNKS // 2) as h:
                    for b in range(2):
                        load(h, b)
            sp.wait_ge(stats_ready, CHUNKS + 1)
            sp.wait_ge(normed_ready, CHUNKS + 1)
            sp.dma_start(total[0:REST, CHUNKS % 4, 0, :], acc[0:REST, :]).then_inc(total_in[0], 16)
            for b in range(2):
                sp.wait_ge(stored[b], 16 * (CHUNKS // 2 + 2 - b))

        @block.gpsimd
        def _(pool):
            pool.memset(src_raw[96:UNITS, :, :], 0).then_inc(cleared, 1)
            pool.iota(dst_raw[96:UNITS, :, :], [[0, G], [1, P]], base=N + 2 * P, channel_multiplier=0
                      ).then_inc(cleared, 1)
            pool.memset(len_raw[96:UNITS, :, :], 0.0).then_inc(cleared, 1)
            pool.memset(vec_raw[96:UNITS, :, :, :], 0.0).then_inc(cleared, 1)
            pool.wait_ge(cleared, 4)
            pool.iota(dump_row[:, :], [[P, 2]], base=N, channel_multiplier=1).then_inc(cleared, 1)
            for a in (up_raw[:, :], mlp0_raw[:, :, :], mlp1[:, :], mlp2[:, :, :]):
                pool.memset(a, 0.0)
            pool.memset(out_raw[:, :, :], 0.0).then_inc(consts, 1)
            for k in range(NB):
                pool.memset(minus_k[:, k:k + 1], float(-k))
            pool.memset(ident[:, :], 0.0)
            pool.memset(backward[:, :], 0.0)
            pool.iota(by_index[:, :], [[1, PAIRS]], base=0, channel_multiplier=0,
                      allow_small_or_imprecise_dtypes=True)
            pool.memset(final[:, :], 0.0)
            pool.memset(dense_orders[:, :], 0)
            pool.memset(meet[:, :], 0.0)
            for a in least:
                pool.memset(a[:, :], float(N))
            pool.memset(earlier[:, :], 1.0).then_inc(consts, 1)
            pool.wait_ge(consts, 2)
            pool.affine_select(out=ident[:, :], in_=ident[:, :], compare_op=ALU.not_equal, fill=1.0,
                               base=0, pattern=[[-1, P]], channel_multiplier=1).then_inc(consts, 1)
            pool.affine_select(out=backward[:, :], in_=backward[:, :], compare_op=ALU.not_equal, fill=1.0,
                               base=1 - UNITS, pattern=[[1, P]], channel_multiplier=1).then_inc(consts, 1)
            pool.affine_select(out=earlier[:, :], in_=earlier[:, :], compare_op=ALU.is_gt, fill=0.0,
                               base=0, pattern=[[-1, P]], channel_multiplier=1).then_inc(consts, 1)

            def stage(s, b, gathers=True, scatters=True, reused=True):
                if reused:
                    pool.wait_ge(gathered[b], 8 * G * ((min(s, UNITS) if isinstance(s, int) else s) - b))
                if scatters:
                    pool.wait_ge(rows_ready, s - LAG + 1)
                first, last = (0 if gathers else 1), (2 if scatters else 1)
                pool.tensor_copy(index_now[:, b, first:last, :], index[:, bass.ds(s, 1), first:last, :]
                                 .rearrange("p s a i -> p (s a) i")).then_inc(pool_staged, 1)

            def step(s, slot, gathers=True, scatters=True, reused=True, by_order=True, following=None):
                v, b, c, msg_slot = s - LAG, slot % 2, (slot + LAG) % 2, (slot - LAG) % RING
                if scatters:
                    order = pool.value_load(scatter_orders[0:1, bass.ds(v, 1)], min_val=4, max_val=4 * PIECES - 1)
                    pool.wait_ge(acc_init[0], 16 * (order // 8) + 16)
                    pool.wait_ge(acc_init[1], 16 * ((order + 4) // 8))
                    meets = [order % 2] + (G - 1) * [(order // 2) % 2]
                pool.wait_ge(pool_staged, s + 1)
                if gathers and reused:
                    pool.wait_ge(senderT_ps, s - RING + 1)
                if scatters:
                    pool.wait_ge(msg_ready, v + 1)
                pool.sem_inc(pool_passed, 1)
                for i in range(G):
                    if gathers:
                        pool.indirect_dma_start(sender[:, slot, i, :], None, x,
                                                bass.IndirectOffsetOnAxis(ap=index_now[:, b, 0, i:i + 1], axis=0)
                                                ).then_inc(gathered[b], 16)
                    if scatters:
                        if i >= 1:
                            before = scattered[c][i - 1], 8 * (v - c) + 16
                        else:
                            before = scattered[1 - c][G - 1], 8 * (v - c) + 16 * c
                        if i >= 2:
                            pool.wait_ge(scattered[c][i - 2], 8 * (v - c) + 16)
                        elif by_order:
                            pool.wait_ge(scattered[1 - c][G - 2 + i], 8 * (v - c) + 16 * c)
                        if by_order:
                            pool.wait_ge(before[0], before[1] - 16 + 16 * meets[i])
                        elif i >= 1 or s > LAG:
                            pool.wait_ge(*before)
                        pool.sem_inc(pool_passed, 1)
                        pool.indirect_dma_start(acc, bass.IndirectOffsetOnAxis(ap=index_now[:, b, 1, i:i + 1], axis=0),
                                                msg[:, msg_slot, i, :], None, compute_op=ALU.add
                                                ).then_inc(scattered[c][i], 16)
                    if i == 1 and following is not None:
                        stage(s + 1, 1 - b, **following)

            pool.wait_ge(index_in, 1)
            stage(0, 0, scatters=False, reused=False)
            for s in range(LAG):
                step(s, s % RING, scatters=False, reused=s >= RING,
                     following=dict(scatters=s + 1 >= LAG, reused=s + 1 >= 2))
            pool.wait_ge(spare_rows, 16)
            pool.wait_ge(scatter_tables, 1)
            rounds = -(-(LAG + 3) // RING), (UNITS - 2) // RING
            for s in range(LAG, rounds[0] * RING):
                step(s, s % RING, by_order=s - LAG >= 3, following={})
            with pool.Fori(*rounds) as j:
                for slot in range(RING):
                    step(RING * j + slot, slot, following={})
            for s in range(UNITS - 2, UNITS + LAG):
                step(s, s % RING, gathers=s < UNITS,
                     following=dict(gathers=s + 1 < UNITS) if s + 1 < UNITS + LAG else None)

        @block.tensor
        def _(pe):
            pe.wait_ge(consts, 5)
            pe.wait_ge(edges_f32, 1)
            pe.wait_ge(edges_in, 16 * 12)
            for a, to in ((src_rawf, ps_src), (dst_rawf, ps_dst), (len_raw, ps_len)):
                for q in range(G):
                    mm = pe.transpose(to[:, q, 0:UNITS], a[:, q, :], backward[0:UNITS, 0:UNITS])
                mm.then_inc(planes, 1)
            for c, to in enumerate(ps_vec):
                for q in range(G):
                    mm = pe.transpose(to[:, q, 0:UNITS], vec_raw[:, q, :, c], backward[0:UNITS, 0:UNITS])
                mm.then_inc(planes, 1)
            pe.wait_ge(tile_ends, 2)
            for a, to in ((low_raw, ps_low), (high_raw, ps_high)):
                for q in range(G):
                    mm = pe.transpose(to[0:1, q, 0:UNITS], a[:, q:q + 1], backward[0:UNITS, 0:UNITS])
                mm.then_inc(ends_ps, 1)
            pe.wait_ge(weights, 6)
            pe.wait_ge(act_planes, 4)
            pe.wait_ge(prepared, 3)
            pe.wait_ge(index_in, 1)
            pe.wait_ge(loaded, 16 * WEIGHT_DMAS)

            def turn(u, k):
                b = k % 2
                pe.wait_ge(basis_staged, u + 1)
                if k >= 1:
                    pe.wait_ge(hid1_ready, u)
                pe.transpose(ps_hid[0:G * NB, 2, :], basis[:, b, :], ident[:, :]).then_inc(basisT_ps, 1)
                if k >= 1:
                    pe.wait_ge(same_ready, u)
                for i in range(G):
                    mm = pe.transpose(ps_dst[:, i, :], dst_now[:, b, i:i + 1].broadcast_to([P, P]), ident[:, :])
                mm.then_inc(dst_ps, 1)
                pe.wait_ge(gathered[b], u * (16 * G // 2) + 16 * G - 16 * G * b // 2)
                if k >= 1:
                    pe.wait_ge(senderT_ready, u)
                for i in range(G):
                    mm = pe.transpose(ps_sT[:, P * i:P * (i + 1)], sender[:, k % RING, i, :], ident[:, :])
                mm.then_inc(senderT_ps, 1)

            def hidden0(u, k):
                b = k % 2
                pe.wait_ge(basisT_ready, u + 1)
                for q in range(2):
                    mm = pe.matmul(ps_hid[:, q, :], mlp0[:, q, :], basisT[:, b, :], start=True, stop=True)
                mm.then_inc(hid0_ps, 1)

            def hidden1(u, k):
                pe.wait_ge(hid0_ready, u + 1)
                pe.matmul(ps_hid[:, 2:4, :], mlp1[:, :], hid0[:, k % 2, :], start=True, stop=True
                          ).then_inc(hid1_ps, 1)

            def project_up(u, k):
                b = k % 2
                pe.wait_ge(senderT_ready, u + 1)
                if k >= 1:
                    pe.wait_ge(up_used, u)
                for i in range(G):
                    mm = pe.matmul(ps_up[:, i, :], senderT[:, b, P * i:P * (i + 1)], up[:, :], start=True, stop=True)
                mm.then_inc(up_ps, 1)

            def radial(u, k):
                b = k % 2
                pe.wait_ge(hid1_ready, u + 1)
                for i in range(G):
                    mm = pe.matmul(ps_wts[:, i, :], hid1[:, b, P * (i // 2):P * (i // 2 + 1)], mlp2[:, i % 2, :],
                                   start=True, stop=True)
                mm.then_inc(wts_ps, 1)

            def sums(v, k, r):
                b = k % 2
                if r == 0:
                    pe.wait_ge(mid_ready, v + 1)
                if k >= 1:
                    pe.wait_ge(sum_ready[r], v)
                for i in range(2):
                    for h in range(2):
                        mm = pe.matmul(ps_sum[r][:, i, h, :], mid[:, b, 2 * r + i, P * h:P * (h + 1)],
                                       same[:, b, 2 * r + i, :], start=True, stop=True)
                mm.then_inc(sum_ps[r], 1)

            def project_out(v, k):
                b = k % 2
                if k >= 1:
                    pe.wait_ge(msg_ready, v)
                for i in range(G):
                    if i % 2 == 0:
                        pe.wait_ge(sum_ready[i // 2], v + 1)
                    for h in range(2):
                        mm = pe.matmul(ps_msg[:, i, 2 * MUL * h:2 * MUL * (h + 1)], sumT[:, b, i, h, :],
                                       outw[:, h, :], start=True, stop=True)
                mm.then_inc(msg_ps, 1)

            def unit(u, k, following=True, tail=False):
                if not tail:
                    hidden0(u, k)
                    project_up(u, k)
                if k >= 1:
                    sums(u - 1, k - 1, 0)
                if not tail:
                    hidden1(u, k)
                if k >= 1:
                    sums(u - 1, k - 1, 1)
                if not tail:
                    radial(u, k)
                if following and not tail:
                    turn(u + 1, k + 1)
                if k >= 1:
                    project_out(u - 1, k - 1)

            turn(0, 0)
            for u in range(RING):
                unit(u, u)
            with pe.Fori(1, (UNITS - 2) // RING) as j:
                for k in range(RING):
                    unit(RING * j + k, RING + k)
            unit(UNITS - 2, UNITS - 2)
            unit(UNITS - 1, UNITS - 1, following=False)
            unit(UNITS, UNITS, tail=True)

        @block.scalar
        def _(act):
            load_edges(act, [(src_raw[:, :, :], src, 1), (len_raw[:, :, :], edge_len, 1)])
            for b in range(2):
                act.dma_start(start[:, b:b + 1], column(b0)).then_inc(stored[b], 16)
            len_units = len_all[:, :].rearrange("p (v i) -> p v i", i=G)
            vec_units = vec_all[:, :, :].rearrange("p (v i) c -> p v i c", i=G)
            for k, (a, to) in enumerate([(ps_len, len_units)] + [(ps_vec[c], vec_units[:, :, :, c]) for c in range(3)]):
                act.wait_ge(planes, 3 + k)
                for w in range(2):
                    mm = act.copy(turns(to, w), row_tiles(a, w))
                mm.then_inc(act_planes, 1)
            act.wait_ge(dve_pre, 3)
            for k in range(NB):
                mm = act.activation(basis_all[:, :, k], len_clip[:, :], ACT.Square, scale=float(NB - 1),
                                    bias=minus_k[:, k:k + 1])
            mm.then_inc(act_pre, 1)
            act.wait_ge(act_pre, 1)
            act.activation(basis_all[:, :, :], basis_all[:, :, :], ACT.Exp, scale=-0.5).then_inc(act_pre, 1)
            act.wait_ge(dve_pre, 5)
            act.activation(norm[:, :], norm[:, :], ACT.Sqrt).then_inc(act_pre, 1)
            act.wait_ge(loaded, 16 * WEIGHT_DMAS)
            act.mul(up[:, :], up_raw[:, :], MUL ** -0.5).then_inc(weights, 1)
            act.mul(mlp0[:, :, :], mlp0_raw[:, :, :], NB ** 0.5).then_inc(weights, 1)
            by = 1.0 / (AVG * (2 * MUL) ** 0.5)
            for k in range(4):
                for h in range(2):
                    rows = slice(MUL * k, MUL * (k + 1))
                    y = 3 ** 0.5 if k == 2 or (k == 0 and h == 1) else 1.0
                    mm = act.mul(outw[rows, h, :], out_raw[rows, h, :], by * y)
                mm.then_inc(weights, 1)

            def stage(u, k):
                b = k % 2
                act.copy(basis[:, b, :].rearrange("p (i k) -> p i k", k=NB), basis_all[:, bass.ds(u * G, G), :])
                act.copy(dst_now[:, b, :], dst_all[:, bass.ds(u, 1), :].rearrange("p v i -> p (v i)")
                         ).then_inc(basis_staged, 1)

            def sums_out(v, k, r):
                b = k % 2
                act.wait_ge(sum_ps[r], v + 1)
                act.copy(sumT[:, b, 2 * r:2 * r + 2, :, :], ps_sum[r][:, :, :, :]).then_inc(sum_ready[r], 1)

            def msg_out(v, k):
                b = k % 2
                act.wait_ge(msg_ps, v + 1)
                slot = bass.ds(v % RING, 1)
                if k >= RING:
                    for i in range(2, G):
                        act.wait_ge(scattered[b][i], 8 * (v - b) - 8 * RING + 16)
                act.copy(msg[:, slot, :, 0:MUL].rearrange("p s i k -> p (s i) k"), ps_msg[:, :, 0:MUL])
                act.copy(msg[:, slot, :, MUL:D].rearrange("p s i (k c) -> p (s i) c k", c=3),
                         ps_msg[:, :, MUL:D].rearrange("p i (c k) -> p i c k", c=3)).then_inc(msg_ready, 1)

            def turned(u, k, stage_next=True):
                b = k % 2
                act.wait_ge(basisT_ps, u + 1)
                act.copy(basisT[:, b, :], ps_hid[0:G * NB, 2, :]).then_inc(basisT_ready, 1)
                act.wait_ge(senderT_ps, u + 1)
                act.copy(senderT[:, b, :], ps_sT[:, :]).then_inc(senderT_ready, 1)
                if stage_next:
                    stage(u + 2, k)

            def silu0(u, k):
                act.wait_ge(hid0_ps, u + 1)
                act.activation(hid0[:, k % 2, :], ps_hid[:, 0:2, :].rearrange("p q e -> p (q e)"), ACT.Silu,
                               bias=bias0[:, :]).then_inc(hid0_ready, 1)

            def unit(u, k, tail=False, meanwhile=None):
                b = k % 2
                if not tail:
                    silu0(u, k)
                if k >= 1:
                    sums_out(u - 1, k - 1, 0)
                if not tail:
                    act.wait_ge(hid1_ps, u + 1)
                    act.activation(hid1[:, b, :], ps_hid[:, 2:4, :].rearrange("p q e -> p (q e)"), ACT.Silu,
                                   bias=bias1[:, :]).then_inc(hid1_ready, 1)
                if k >= 1:
                    sums_out(u - 1, k - 1, 1)
                if meanwhile is not None:
                    meanwhile()
                if not tail and not (isinstance(u, int) and u + 1 >= UNITS):
                    turned(u + 1, k + 1, stage_next=not isinstance(u, int) or u + 3 < UNITS)
                if k >= 1:
                    msg_out(u - 1, k - 1)

            act.wait_ge(prepared, 4)
            act.wait_ge(act_pre, 2)
            act.sem_inc(stats_ready, 2)
            act.sem_inc(normed_ready, 4)

            def normalise(h, b, part, rows=ROWS, parts=P, store=False):
                c = 2 * h + b
                if part == 0:
                    act.wait_ge(shift_ready, c + 1)
                    act.wait_ge(stored[b], 16 * h + 16)
                quarter = bass.ds(2 * (h % 2) + b, 1)
                half = (rows + 1) // 2
                for r in (range(half, rows) if part else range(half)):
                    mm = act.activation(normed[0:parts, b, r, :],
                                        total[0:parts, quarter, r, :].rearrange("p b d -> p (b d)"), ACT.Identity,
                                        scale=rstd[0:parts, b, r:r + 1], bias=shift[0:parts, b, r:r + 1])
                if part == 0 and rows > 1:
                    return
                mm.then_inc(normed_ready, 1)
                if not store:
                    return
                act.wait_ge(normed_ready, c + 5)
                if parts == P:
                    to = out[bass.ds(N - CHUNK - c * CHUNK, CHUNK), :].rearrange("(p r) d -> p (r d)", p=P)
                    act.dma_start(to, normed[:, b, :, :].rearrange("p r d -> p (r d)")).then_inc(stored[b], 16)
                else:
                    act.dma_start(out[0:parts, :], normed[0:parts, b, 0, :]).then_inc(stored[b], 16)

            def pair(j, k):
                order = act.value_load(dense_orders[0:1, bass.ds(j, 1)], min_val=0, max_val=2 * CHUNKS - 2)
                for part in range(2):
                    def dense():
                        for b in range(2):
                            with act.If((order // 2 if b else order) % 2):
                                normalise(order // 4, b, part)

                    unit(2 * j + part, k + part, meanwhile=dense)

            stage(0, 0)
            stage(1, 1)
            turned(0, 0)
            first = RING // 2 + 1
            for u in range(2 * first):
                unit(u, u)
            act.wait_ge(tables, 1)
            with act.Fori(first, PAIRS - 2) as j:
                pair(j, 2 * first)
            for j in range(PAIRS - 2, PAIRS):
                pair(j, 2 * j)
            unit(UNITS, UNITS, tail=True)
            done = act.value_load(done_count[0:1, 2:3], min_val=0, max_val=CHUNKS - 1)
            with act.If(done % 2):
                for part in range(2):
                    normalise(done // 2, 1, part, store=True)
            with act.If(CHUNKS - 1 - done):
                with act.Fori((done + 1) // 2, CHUNKS // 2) as h:
                    for b in range(2):
                        for part in range(2):
                            normalise(h, b, part, store=True)
            normalise(CHUNKS // 2, 0, 0, 1, REST, store=True)

        @block.vector
        def _(dve):
            dve.memset(zeros[:, :, :], 0.0).then_inc(zeroed, 1)
            dve.wait_ge(edges_in, 16 * 12)
            dve.tensor_copy(src_rawf[:, :, :], src_raw[:, :, :])
            dve.tensor_copy(dst_rawf[:, :, :], dst_raw[:, :, :]).then_inc(edges_f32, 1)
            dve.wait_ge(edges_f32, 1)
            dve.tensor_reduce(low_raw[:, :], dst_rawf[:, :, :], AX_X, ALU.min).then_inc(tile_ends, 1)
            dve.tensor_reduce(high_raw[:, :], dst_rawf[:, :, :], AX_X, ALU.max).then_inc(tile_ends, 1)
            dve.wait_ge(planes, 1)
            for w in range(2):
                mm = dve.tensor_copy(turns(index[:, 0:UNITS, 0, :], w), row_tiles(ps_src, w))
            mm.then_inc(index_in, 1)
            dve.wait_ge(planes, 2)
            for w in range(2):
                dve.tensor_copy(turns(dst_all[:, :, :], w), row_tiles(ps_dst, w)).then_inc(prepared, 1)
            dve.wait_ge(ends_ps, 2)
            for w in range(2):
                dve.tensor_scalar(turns(low[:, :, :], w), row_tiles(ps_high[0:1, :, :], w), -1.0, float(N - 1),
                                  ALU.mult, ALU.add)
                mm = dve.tensor_scalar(turns(high[:, :, :], w), row_tiles(ps_low[0:1, :, :], w), -1.0, float(N - 1),
                                       ALU.mult, ALU.add)
            mm.then_inc(prepared, 1)
            dve.wait_ge(act_planes, 4)
            dve.tensor_copy(dump_rowf[:, :], dump_row[:, :]).then_inc(dump_ready, 1)
            dve.wait_ge(prepared, 2)
            dve.wait_ge(dump_ready, 1)
            dve.tensor_tensor(gap_all[:, :, :].rearrange("p v (h r) -> p (v h) r", r=2),
                              wide(dump_rowf[:, :], 1, TILES // 2),
                              dst_all[:, :, :].rearrange("p v (h r) -> p (v h) r", r=2), ALU.subtract
                              ).then_inc(prepared, 1)

            dve.wait_ge(act_planes, 4)
            dve.tensor_scalar(len_clip[:, :], len_all[:, :], 0.0, 1.0, ALU.max, ALU.min).then_inc(dve_pre, 1)
            dve.tensor_scalar(beyond[:, :], len_all[:, :], 1.0, FAR, ALU.is_gt, ALU.mult).then_inc(dve_pre, 1)
            dve.wait_ge(dve_pre, 2)
            dve.tensor_tensor(len_clip[:, :], len_clip[:, :], beyond[:, :], ALU.add).then_inc(dve_pre, 1)
            dve.tensor_tensor(vec_sq[:, :, :], vec_all[:, :, :], vec_all[:, :, :], ALU.mult).then_inc(dve_pre, 1)
            dve.wait_ge(dve_pre, 4)
            dve.tensor_reduce(norm[:, :], vec_sq[:, :, :], AX_X, ALU.add).then_inc(dve_pre, 1)

            def directions():
                dve.wait_ge(act_pre, 3)
                dve.tensor_scalar(norm[:, :], norm[:, :], 1e-12, None, ALU.add).then_inc(dve_pre, 1)
                dve.wait_ge(dve_pre, 6)
                dve.reciprocal(norm[:, :], norm[:, :]).then_inc(dve_pre, 1)
                dve.wait_ge(dve_pre, 7)
                dve.tensor_tensor(vec_all[:, :, :], vec_all[:, :, :], wide(norm[:, :], 2, 3), ALU.mult
                                  ).then_inc(directions_ready, 1)
                dve.wait_ge(directions_ready, 1)

            steps = [0]

            def link(ins):
                steps[0] += 1
                ins.then_inc(table_step, 1)
                dve.wait_ge(table_step, steps[0])

            def floor_div(out, of, by, shift):
                n = out.shape[-1]
                link(dve.tensor_scalar(floor_int[:, 0:n], of, shift, 1.0 / by, ALU.add, ALU.mult))
                link(dve.tensor_copy(out, floor_int[:, 0:n]))
                link(dve.scalar_tensor_tensor(out=too_much[:, 0:n], in0=out, scalar=float(by), in1=of, op0=ALU.mult,
                                              op1=ALU.is_gt))
                link(dve.tensor_tensor(out, out, too_much[:, 0:n], ALU.subtract))

            def make_scatter_orders():
                lo, hi = (a[:, :, :].rearrange("p v i -> p (v i)") for a in (low, high))
                by_unit = meet[:, :].rearrange("p (v i) -> p v i", i=G)
                link(dve.tensor_tensor(meet[:, 1:TILES], hi[:, 0:TILES - 1], lo[:, 1:TILES], ALU.is_ge))
                link(dve.tensor_tensor(meet_too[:, 1:TILES], hi[:, 1:TILES], lo[:, 0:TILES - 1], ALU.is_ge))
                link(dve.tensor_tensor(meet[:, 1:TILES], meet[:, 1:TILES], meet_too[:, 1:TILES], ALU.mult))
                link(dve.tensor_reduce(meet_unit[:, :], by_unit[:, :, 1:G], AX_X, ALU.max))
                link(dve.tensor_reduce(deepest[:, :], high[:, :, :], AX_X, ALU.max))
                floor_div(pieces[:, :], deepest[:, :], PIECE, 0.5)
                link(dve.tensor_scalar(pieces[:, :], pieces[:, :], 1.0, float(PIECES - 1), ALU.max, ALU.min))
                link(dve.tensor_scalar(pieces[:, :], pieces[:, :], 4.0, None, ALU.mult))
                link(dve.scalar_tensor_tensor(out=orders[:, :], in0=meet_unit[:, :], scalar=2.0, in1=pieces[:, :],
                                              op0=ALU.mult, op1=ALU.add))
                dve.tensor_tensor(scatter_orders[:, :], orders[:, :], by_unit[:, :, 0], ALU.add
                                  ).then_inc(scatter_tables, 1)

            def make_dense_orders():
                link(dve.tensor_reduce(least[0][:, 0:UNITS], low[:, :, :], AX_X, ALU.min))
                link(dve.tensor_copy(least[1][:, 0:UNITS], least[0][:, 1:UNITS + 1]))
                now, reach = 1, 1
                while reach < UNITS:
                    link(dve.tensor_tensor(least[1 - now][:, 0:UNITS], least[now][:, 0:UNITS],
                                           least[now][:, reach:UNITS + reach], ALU.min))
                    now, reach = 1 - now, 2 * reach
                by_pair = least[now][:, 0:UNITS].rearrange("p (j b) -> p j b", b=2)[:, :, 1]
                floor_div(rising[:, :], by_pair, CHUNK, 0.5)
                link(dve.tensor_scalar(rising[:, :], rising[:, :], float(CHUNKS - 1), None, ALU.min))
                link(dve.memset(rising[:, 0:DENSE_FROM], 0.0))
                link(dve.scalar_tensor_tensor(out=least[0][:, AT:AT + PAIRS], in0=by_index[:, :], scalar=-RATE,
                                              in1=rising[:, :], op0=ALU.mult, op1=ALU.add))
                now, reach = 0, 1
                while reach < PAIRS:
                    link(dve.tensor_tensor(least[1 - now][:, AT:AT + PAIRS], least[now][:, AT:AT + PAIRS],
                                           least[now][:, AT - reach:AT + PAIRS - reach], ALU.min))
                    now, reach = 1 - now, 2 * reach
                link(dve.scalar_tensor_tensor(out=least[now][:, AT:AT + PAIRS], in0=by_index[:, :], scalar=RATE,
                                              in1=least[now][:, AT:AT + PAIRS], op0=ALU.mult, op1=ALU.add))
                floor_div(final[:, 1:1 + PAIRS], least[now][:, AT:AT + PAIRS], 1, 0.1)
                for k, after in enumerate((0, STATS_AFTER, NORM_AFTER)):
                    dve.tensor_copy(done_count[:, k:k + 1], final[:, PAIRS - after:PAIRS - after + 1])
                link(dve.tensor_tensor(fresh[:, :], final[:, 1:1 + PAIRS], final[:, 0:PAIRS], ALU.subtract))
                link(dve.tensor_scalar(rising[:, :], final[:, 1:1 + PAIRS], -1.0, 0.0, ALU.add, ALU.max))
                floor_div(half_chunk[:, :], rising[:, :], 2, 0.5)
                link(dve.scalar_tensor_tensor(out=rising[:, :], in0=half_chunk[:, :], scalar=-2.0, in1=rising[:, :],
                                              op0=ALU.mult, op1=ALU.add))
                link(dve.scalar_tensor_tensor(out=fresh[:, :], in0=rising[:, :], scalar=1.0, in1=fresh[:, :],
                                              op0=ALU.add, op1=ALU.mult))
                dve.scalar_tensor_tensor(out=dense_orders[:, NORM_AFTER:NORM_AFTER + PAIRS], in0=half_chunk[:, :],
                                         scalar=4.0, in1=fresh[:, :], op0=ALU.mult, op1=ALU.add).then_inc(tables, 1)
                dve.wait_ge(tables, 1)

            make_scatter_orders()
            dve.wait_ge(loaded, 16 * WEIGHT_DMAS)

            def equal_receivers(u, k):
                b = k % 2
                dst_col = dst_all[:, bass.ds(u, 1), :].rearrange("p v i -> p (v i)")
                dve.wait_ge(dst_ps, u + 1)
                if k >= 2:
                    dve.wait_ge(sum_ps[1], u - 1)
                dve.tensor_tensor(same[:, b, :, :], ps_dst[:, :, :], wide(dst_col, 2, P), ALU.is_equal
                                  ).then_inc(same_ready, 1)
                dve.wait_ge(same_ready, u + 1)
                for i in range(G):
                    mm = dve.tensor_tensor_reduce(junk[:, b, i, :], same[:, b, i, :], earlier[:, :], 1.0, 0.0,
                                                  ALU.mult, ALU.add, count[:, b, i:i + 1])
                mm.then_inc(counted, 1)

            def receiver_rows(u, k, step):
                b = k % 2
                if step == 0:
                    dve.wait_ge(counted, u + 1)
                    dve.scalar_tensor_tensor(out=rowf[:, b, :], in0=count[:, b, :], scalar=1.0,
                                             in1=gap_all[:, bass.ds(u, 1), :].rearrange("p v i -> p (v i)"),
                                             op0=ALU.min, op1=ALU.mult).then_inc(rowf_ready, 1)
                else:
                    dve.wait_ge(rowf_ready, u + 1)
                    dve.tensor_tensor(index[:, bass.ds(u + LAG, 1), 1, :].rearrange("p s i -> p (s i)"),
                                      rowf[:, b, :], dst_all[:, bass.ds(u, 1), :].rearrange("p v i -> p (v i)"),
                                      ALU.add).then_inc(rows_ready, 1)

            def products(u, k):
                b = k % 2
                y = vec_all[:, bass.ds(u * G, G), :]
                w, md = wts[:, b, :, :], mid[:, b, :, :]
                s, v = ps_up[:, :, 0:MUL], ps_up[:, :, MUL:D].rearrange("p i (c k) -> p i c k", c=3)
                pairs = md[:, :, 0:8 * MUL].rearrange("p i (c k) -> p i c k", c=4)
                pj = proj[:, b, :, :].rearrange("p i (c k) -> p i c k", c=3)
                dve.wait_ge(up_ps, u + 1)
                dve.tensor_tensor(pj, v, wide(y, 3, MUL), ALU.mult).then_inc(dve_step, 1)
                receiver_rows(u, k, 0)
                dve.wait_ge(dve_step, 2 * u + 1)
                dve.tensor_reduce(dot[:, b, :, :], pj.rearrange("p i c k -> p i k c"), AX_X, ALU.add
                                  ).then_inc(dve_step_dot, 1)
                receiver_rows(u, k, 1)
                dve.wait_ge(wts_ps, u + 1)
                dve.tensor_tensor(w, ps_wts[:, :, :], wide(bias2[:, :], 1, G), ALU.add).then_inc(wts_ready, 1)
                dve.wait_ge(wts_ready, u + 1)
                dve.tensor_tensor(md[:, :, 8 * MUL:9 * MUL], w[:, :, MUL:2 * MUL], s, ALU.mult
                                  ).then_inc(dve_step, 1)
                dve.tensor_tensor(md[:, :, 0:MUL], w[:, :, 0:MUL], s, ALU.mult)
                dve.tensor_tensor(pairs[:, :, 1:4, MUL:2 * MUL], v, wide(w[:, :, 2 * MUL:3 * MUL], 2, 3), ALU.mult
                                  ).then_inc(up_used, 1)
                dve.wait_ge(dve_step, 2 * u + 2)
                dve.tensor_tensor(pairs[:, :, 1:4, 0:MUL], wide(md[:, :, 8 * MUL:9 * MUL], 2, 3), wide(y, 3, MUL),
                                  ALU.mult)
                dve.wait_ge(dve_step_dot, u + 1)
                dve.tensor_tensor(md[:, :, MUL:2 * MUL], w[:, :, 3 * MUL:D], dot[:, b, :, :], ALU.mult
                                  ).then_inc(mid_ready, 1)

            def unit(u, k, following=True):
                products(u, k)
                if following:
                    equal_receivers(u + 1, k + 1)

            def moments(h, b, rows=ROWS, parts=P):
                c = 2 * h + b
                quarter = bass.ds(2 * (h % 2) + b, 1)
                dve.wait_ge(total_in[b], 16 * h + 16)
                for r in range(rows):
                    mm = dve.bn_stats(stats[0:parts, r, :], total[0:parts, quarter, r, :].rearrange("p b d -> p (b d)"))
                mm.then_inc(stats_ready, 1)

            def statistics(h, b, rows=ROWS, parts=P):
                c = 2 * h + b
                st = stats[0:parts, 0:rows, :]
                mn, hg, gs = (a[0:parts, 0:rows] for a in (mean, half_gap, gap_sq))
                vr, rs, sh, bt = (a for a in (var[0:parts, 0:rows], rstd[0:parts, b, 0:rows],
                                              shift[0:parts, b, 0:rows], bits[0:parts, 0:rows]))
                step = SSTEPS * c
                dve.wait_ge(stats_ready, c + 3)
                dve.tensor_tensor(mn, st[:, :, 1], st[:, :, 4], ALU.add)
                dve.tensor_tensor(vr, st[:, :, 2], st[:, :, 5], ALU.add)
                dve.tensor_tensor(hg, st[:, :, 1], st[:, :, 4], ALU.subtract).then_inc(stat_step, 1)
                dve.wait_ge(stat_step, step + 1)
                dve.scalar_tensor_tensor(out=gs, in0=hg, scalar=0.25, in1=hg, op0=ALU.mult, op1=ALU.mult)
                dve.tensor_scalar(vr, vr, 1.0 / D, EPS, ALU.mult, ALU.add).then_inc(stat_step, 1)
                dve.wait_ge(stat_step, step + 2)
                dve.tensor_tensor(vr, vr, gs, ALU.add).then_inc(stat_step, 1)
                dve.wait_ge(stat_step, step + 3)
                dve.tensor_scalar(bt, vr.bitcast(I32), 1, None, ALU.logical_shift_right).then_inc(stat_step, 1)
                dve.wait_ge(stat_step, step + 4)
                dve.wait_ge(normed_ready, c + 3)
                dve.tensor_scalar(rs.bitcast(I32), bt, -1.0, RSQRT_BITS, ALU.mult, ALU.add).then_inc(stat_step, 1)
                for k in range(ROUNDS):
                    dve.wait_ge(stat_step, step + 5 + 3 * k)
                    dve.tensor_tensor(gs, rs, rs, ALU.mult).then_inc(stat_step, 1)
                    dve.wait_ge(stat_step, step + 6 + 3 * k)
                    dve.scalar_tensor_tensor(out=gs, in0=gs, scalar=-0.5, in1=vr, op0=ALU.mult, op1=ALU.mult
                                             ).then_inc(stat_step, 1)
                    dve.wait_ge(stat_step, step + 7 + 3 * k)
                    dve.scalar_tensor_tensor(out=rs, in0=gs, scalar=1.5, in1=rs, op0=ALU.add, op1=ALU.mult
                                             ).then_inc(stat_step, 1)
                dve.wait_ge(stat_step, step + SSTEPS)
                dve.scalar_tensor_tensor(out=sh, in0=mn, scalar=-0.5, in1=rs, op0=ALU.mult, op1=ALU.mult
                                         ).then_inc(shift_ready, 1)

            def pair(j, k, last=False):
                order = dve.value_load(dense_orders[0:1, bass.ds(j + NORM_AFTER - STATS_AFTER, 1)], min_val=0,
                                       max_val=2 * CHUNKS - 2)
                for part in range(2):
                    unit(2 * j + part, k + part, following=part == 0 or not last)
                    for b in range(2):
                        with dve.If((order // 2 if b else order) % 2):
                            (statistics if part else moments)(order // 4, b)

            directions()
            equal_receivers(0, 0)
            unit(0, 0)
            unit(1, 1)
            make_dense_orders()
            with dve.Fori(1, PAIRS - 1) as j:
                pair(j, 4)
            pair(PAIRS - 1, UNITS - 2, last=True)
            done = dve.value_load(done_count[0:1, 1:2], min_val=0, max_val=CHUNKS - 1)
            with dve.If(done % 2):
                moments(done // 2, 1)
                statistics(done // 2, 1)
            with dve.If(CHUNKS - 1 - done):
                with dve.Fori((done + 1) // 2, CHUNKS // 2) as h:
                    for b in range(2):
                        moments(h, b)
                        statistics(h, b)
            moments(CHUNKS // 2, 0, 1, REST)
            statistics(CHUNKS // 2, 0, 1, REST)


_INS = ['x', 'src', 'dst', 'edge_attr_3', 'edge_weight', 'L0_gnn_W_up0', 'L0_gnn_W_up1', 'L0_gnn_mlp_w0',
        'L0_gnn_mlp_b0', 'L0_gnn_mlp_w1', 'L0_gnn_mlp_b1', 'L0_gnn_mlp_w2', 'L0_gnn_mlp_b2', 'L0_gnn_W_out0',
        'L0_gnn_W_out1']


def kernel(**inputs):
    import numpy as _np
    import concourse.bacc as _bacc
    from concourse import mybir as _mybir
    from concourse.bass_utils import run_bass_kernel_spmd as _run

    nc = _bacc.Bacc("TRN2", target_bir_lowering=False, num_devices=1)
    arrays, args = {}, []
    for name in _INS:
        a = _np.ascontiguousarray(inputs[name])
        arrays[f"in_{name}_dram"] = a
        args.append(nc.dram_tensor(f"in_{name}_dram", a.shape, _mybir.dt.from_np(a.dtype), kind="ExternalInput").ap())
    args.append(nc.dram_tensor("out_0_dram", (N, D), F32, kind="ExternalOutput").ap())
    bass_gnn(nc, *args)
    r = _run(nc, [arrays], core_ids=[0])
    return r.results[0]["out_0_dram"]
```
